# Optimizing a Trainium2 kernel written in Bass

```python
import numpy as np
import jax
import jax.numpy as jnp

def _softmax(x, axis=-1):
    return jax.nn.softmax(x, axis=axis)

def _gelu(x):
    return jax.nn.gelu(x, approximate=True)

def _silu(x):
    return jax.nn.silu(x)

def _sigmoid(x):
    return jax.nn.sigmoid(x)

def _layernorm(x, axis=-1, eps=1e-05):
    m = jnp.mean(x, axis=axis, keepdims=True)
    v = jnp.var(x, axis=axis, keepdims=True)
    return (x - m) / jnp.sqrt(v + eps)

def _scatter_add(tgt, idx, src, axis=0):
    return tgt.at[idx].add(src)

def _segment_sum(src, seg, n):
    return jax.ops.segment_sum(src, seg, n)
kernel_name = 'mk_gnn_resnorm_d2_gnn_r32_7043e0'

def setup_inputs(seed: int=0):
    np.random.seed(seed)
    _w = jnp.asarray

    def _rec_inputs():
        import jax
        import jax.numpy as jnp
        _gk = jax.random.key(seed)
        x = -0.0001884 + 1 * jax.random.normal(jax.random.fold_in(_gk, 1), (3125, 256), jnp.float32)
        src = jax.random.randint(jax.random.fold_in(_gk, 2), (50000,), 0, 3125, jnp.int32)
        dst = jnp.minimum((3125 * jax.random.uniform(jax.random.fold_in(_gk, 3), (50000,)) ** 2.0).astype(jnp.int32), 99999)
        _o = jnp.argsort(dst, stable=True)
        src = src[_o]
        dst = dst[_o]
        edge_type_4 = jax.random.randint(jax.random.fold_in(_gk, 13), (50000,), 0, 4, jnp.int32)
        edge_weight = -0.000423496 + 0.100023 * jax.random.normal(jax.random.fold_in(_gk, 14), (50000,), jnp.float32)
        return (x, src, dst, edge_type_4, edge_weight)
    x, src, dst, edge_type_4, edge_weight = _rec_inputs()

    def _L0_gnn_setup():
        import jax, jax.numpy as jnp
        import numpy as np
        BLOCK_DIMS = [8] * 32

        def _mask_indices():
            d = sum(BLOCK_DIMS)
            mask = np.ones((d, d), dtype=np.int8)
            off = 0
            for b in BLOCK_DIMS:
                mask[off:off + b, off:off + b] = 0
                off += b
            rows, cols = np.nonzero(mask)
            return (d, rows.astype(np.int32), cols.astype(np.int32))
        key = jax.random.key(seed)
        k1, k2 = jax.random.split(key)
        d, rows, cols = _mask_indices()
        N = 15625
        X = jax.random.normal(k1, (N, d), dtype=jnp.float32)
        w_est = 0.1 * jax.random.normal(k2, (rows.shape[0],), dtype=jnp.float32)
        return {'X': X, 'w_est': w_est, 'rows': jnp.asarray(rows), 'cols': jnp.asarray(cols)}
    _L0_gnn_all = _L0_gnn_setup()
    _L0_gnn_in = {k: v for k, v in _L0_gnn_all.items() if k in ()}
    del _L0_gnn_all

    def _L1_gnn_setup():
        import jax, jax.numpy as jnp
        import numpy as np
        N_NODES = 50000
        N_EDGES = 25000
        DIM = 256
        DEPTH = 4
        N_REL = 4
        EPS = 1e-05

        def _rgcn_layer(X, W, root, bias, gamma, beta, src, dst, etype, inv_deg):
            h = jnp.einsum('ni,rio->rno', X, W)
            msg = h[etype, src] * inv_deg[:, None]
            agg = jax.ops.segment_sum(msg, dst, num_segments=X.shape[0])
            out = agg + X @ root + bias
            mu = jnp.mean(out, axis=-1, keepdims=True)
            var = jnp.mean(jnp.square(out - mu), axis=-1, keepdims=True)
            out = (out - mu) * jax.lax.rsqrt(var + EPS) * gamma + beta
            out = jax.nn.elu(out)
            return out + X
        key = jax.random.key(seed)
        ks = jax.random.split(key, 8)
        scale = 1.0 / np.sqrt(DIM)
        return {'node_embedding': jax.random.normal(ks[0], (N_NODES, DIM), jnp.float32), 'weights': jax.random.normal(ks[1], (DEPTH, N_REL, DIM, DIM), jnp.float32) * scale, 'roots': jax.random.normal(ks[2], (DEPTH, DIM, DIM), jnp.float32) * scale, 'biases': jax.random.normal(ks[3], (DEPTH, DIM), jnp.float32) * 0.01, 'ln_gamma': jnp.ones((DEPTH, DIM), jnp.float32), 'ln_beta': jnp.zeros((DEPTH, DIM), jnp.float32), 'edge_index': jax.random.randint(ks[4], (2, N_EDGES), 0, N_NODES, jnp.int32), 'edge_type': jax.random.randint(ks[5], (N_EDGES,), 0, N_REL, jnp.int32)}
    _L1_gnn_all = _L1_gnn_setup()
    _L1_gnn_in = {k: v for k, v in _L1_gnn_all.items() if k in ('weights', 'roots', 'biases', 'ln_gamma', 'ln_beta')}
    del _L1_gnn_all
    return {'x': x, 'src': src, 'dst': dst, 'edge_type_4': edge_type_4, 'edge_weight': edge_weight, 'L1_gnn_weights': _L1_gnn_in['weights'], 'L1_gnn_roots': _L1_gnn_in['roots'], 'L1_gnn_biases': _L1_gnn_in['biases'], 'L1_gnn_ln_gamma': _L1_gnn_in['ln_gamma'], 'L1_gnn_ln_beta': _L1_gnn_in['ln_beta']}

def reference(x, src, dst, edge_type_4, edge_weight, L1_gnn_weights, L1_gnn_roots, L1_gnn_biases, L1_gnn_ln_gamma, L1_gnn_ln_beta):
    import jax
    import jax.numpy as jnp

    def _L0_gnn_ref(X, w_est, rows, cols):
        import jax, jax.numpy as jnp
        import numpy as np
        BLOCK_DIMS = [8] * 32

        def _mask_indices():
            d = sum(BLOCK_DIMS)
            mask = np.ones((d, d), dtype=np.int8)
            off = 0
            for b in BLOCK_DIMS:
                mask[off:off + b, off:off + b] = 0
                off += b
            rows, cols = np.nonzero(mask)
            return (d, rows.astype(np.int32), cols.astype(np.int32))
        d = X.shape[1]
        W = jnp.zeros((d, d), dtype=X.dtype).at[rows, cols].set(w_est)
        return X @ W

    def _L1_gnn_ref(node_embedding, weights, roots, biases, ln_gamma, ln_beta, edge_index, edge_type):
        import jax, jax.numpy as jnp
        import numpy as np
        N_NODES = 50000
        N_EDGES = 25000
        DIM = 256
        DEPTH = 4
        N_REL = 4
        EPS = 1e-05

        def _rgcn_layer(X, W, root, bias, gamma, beta, src, dst, etype, inv_deg):
            h = jnp.einsum('ni,rio->rno', X, W)
            msg = h[etype, src] * inv_deg[:, None]
            agg = jax.ops.segment_sum(msg, dst, num_segments=X.shape[0])
            out = agg + X @ root + bias
            mu = jnp.mean(out, axis=-1, keepdims=True)
            var = jnp.mean(jnp.square(out - mu), axis=-1, keepdims=True)
            out = (out - mu) * jax.lax.rsqrt(var + EPS) * gamma + beta
            out = jax.nn.elu(out)
            return out + X
        src, dst = (edge_index[0], edge_index[1])
        cnt = jnp.zeros((node_embedding.shape[0], N_REL), node_embedding.dtype)
        cnt = cnt.at[dst, edge_type].add(1.0)
        inv_deg = 1.0 / jnp.maximum(cnt[dst, edge_type], 1.0)
        X = node_embedding
        for l in range(DEPTH):
            X = _rgcn_layer(X, weights[l], roots[l], biases[l], ln_gamma[l], ln_beta[l], src, dst, edge_type, inv_deg)
        return X
    edge_index = jnp.stack([src, dst])
    x = _layernorm(x + _L0_gnn_ref(x, edge_weight, src, dst), axis=-1)
    x = _layernorm(x + _L1_gnn_ref(x, L1_gnn_weights, L1_gnn_roots, L1_gnn_biases, L1_gnn_ln_gamma, L1_gnn_ln_beta, edge_index, edge_type_4), axis=-1)
    return x

_drawn_inputs = setup_inputs


def setup_inputs(seed=0):
    import zlib

    import numpy as np

    out = dict(_drawn_inputs(seed))
    spreads = {'L1_gnn_ln_gamma': (1.0, 0.2), 'L1_gnn_ln_beta': (0.0, 0.1)}
    factors = {'L1_gnn_biases': 8.0}
    for name, (base, spread) in spreads.items():
        noise = np.random.default_rng([zlib.crc32(name.encode()), seed]).standard_normal(out[name].shape)
        drawn = base * np.exp(spread * noise) if base else spread * noise
        out[name] = jnp.asarray(drawn.astype(out[name].dtype))
    for name, factor in factors.items():
        out[name] = (out[name] * factor).astype(out[name].dtype)
    return out
```

```python
import concourse.bass as bass
from concourse import mybir
from contextlib import ExitStack

F32 = mybir.dt.float32
I32 = mybir.dt.int32
BF16 = mybir.dt.bfloat16
ALU = mybir.AluOpType
ACT = mybir.ActivationFunctionType
AX = mybir.AxisListType

P = 128
N = 3125
D = 256
E = 50000
L = 4
R = 4
NT = -(-N // P)
NP = NT * P
J = 4
GE = J * P
NG = -(-E // GE)
RG = 7
assert NG % RG == 0
SLOTS = RG * J
CYC = NG // RG
KH = D // P
EPS = 1e-5
KEY = 4096
BIAS = 8 * J
NB = 5 * D

T_LO, T_HI, T_SB, T_GB = 0, 32, 64, 96
T_LM, T_LG, T_LC, T_P, T_REL = 128, 132, 136, 140, 144
T_END = T_REL + NG


def program(nc, x, src, dst, etype, eweight, weights, roots, biases, gammas, betas, out):
    h_rows = [nc.dram_tensor(f"h_rows{i}", [NP, R * D], F32, kind="Internal").ap() for i in range(2)]

    x1_rows = nc.dram_tensor("x1_rows", [P, NT * D], F32, kind="Internal").ap()

    ctx = ExitStack()
    with ctx:
        def sb(name, shape, dt=F32):
            return ctx.enter_context(nc.sbuf_tensor(name, shape, dt))

        def pb(name):
            return ctx.enter_context(nc.psum_tensor(name, [P, 512], F32))

        def sem(name):
            return ctx.enter_context(nc.semaphore(name))

        X = sb("X", [P, NT, D])
        base = sb("base", [P, NT, D])
        wts = sb("wts", [P, L, KH, NB])
        x1 = wts[:].rearrange("p l k n -> p (l k n)")[:, 0:NT * D].rearrange("p (t d) -> p t d", d=D)
        ring = sb("ring", [P, SLOTS, D])
        ringf = ring[:].rearrange("p s d -> p (s d)")
        bias_b = sb("bias_b", [P, L, D])
        gamma_b = sb("gamma_b", [P, L, D])
        beta_b = sb("beta_b", [P, L, D])
        nat_dst_i = ringf[0:NG, 0:512].bitcast(I32)
        nat_src_i = ringf[0:NG, 512:1024].bitcast(I32)
        nat_typ_i = ringf[0:NG, 1024:1536].bitcast(I32)
        nat_w = ringf[0:NG, 1536:2048]
        nat_src = ringf[0:NG, 2048:2560]
        nat_typ = ringf[0:NG, 2560:3072]
        nat_idx = ringf[0:NG, 3072:3584]
        nat_key = ringf[0:NG, 3584:4096]
        key_row = ringf[0:NG, 4096:4608]
        later = ringf[:, 4608:5120]
        OS = ringf[:, 5120:6144].rearrange("p (j n) -> p j n", j=J)
        OD = ringf[:, 6144:7168].rearrange("p (j c n) -> p j c n", j=J, c=2)
        nat_dst = sb("nat_dst", [NG, GE])
        dst_row = sb("dst_row", [NG, GE])
        ecol = sb("ecol", [P, NG, 4, J])
        idx = sb("idx", [P, NG * J], I32)
        ixb = sb("ixb", [P, SLOTS], I32)
        toh = sb("toh", [P, NG, J, R])
        gcol = sb("gcol", [P, 4, J])
        gdi = sb("gdi", [P, 2, J])
        S = sb("S", [P, J, P])
        ST = sb("ST", [P, GE])
        Wm = sb("Wm", [P, KH, D])
        dupw = sb("dupw", [P, GE * (J + 1) // 2], BF16)
        dup = sb("dup", [P, J])
        wlast = sb("wlast", [P, J])
        junk = sb("junk", [P, GE])
        ident = sb("ident", [P, P])
        ones = sb("ones", [P, P])
        iota = sb("iota", [P, D])
        iota_t = sb("iota_t", [P, P])
        pidx = sb("pidx", [P, 1])
        pnode = sb("pnode", [P, NT])
        tbase = sb("tbase", [P, NT])
        tri = sb("tri", [P, NT])
        grow = sb("grow", [P, NG])
        nxt_i = sb("nxt_i", [NG, 1], I32)
        nxt = sb("nxt", [NG, 1])
        cmp = sb("cmp", [NG, 64])
        bad = sb("bad", [NG, 3])
        colv = sb("colv", [NT, 16])
        rowv = sb("rowv", [1, 8])
        relr = sb("relr", [1, NG])
        relr2 = sb("relr2", [1, NG])
        lscr = sb("lscr", [1, L])
        zeros = sb("zeros", [P, D], BF16)
        xcur = sb("xcur", [P, D])
        xo = sb("xo", [P, D])
        ysum = sb("ysum", [P, D])
        z2 = sb("z2", [P, D])
        z3 = sb("z3", [P, D])
        relw = sb("relw", [NT, NG])
        relx = sb("relx", [NT, NG])
        tabf = sb("tabf", [1, T_END])
        tab = sb("tab", [1, T_END], I32)
        invd = sb("invd", [P, R])
        cntm = sb("cntm", [P, R])
        prod = sb("prod", [P, J, R])
        psum4 = sb("psum4", [P, J])
        y = sb("y", [P, D])
        z = sb("z", [P, D])
        zm = sb("zm", [P, D])
        ze = sb("ze", [P, D])
        xn = sb("xn", [P, D])
        xnT = sb("xnT", [P, KH, P])
        xT = sb("xT", [P, KH, P])
        hst = sb("hst", [P, R * D])
        yo = sb("yo", [P, D])
        st6 = sb("st6", [P, 6])
        mv = sb("mv", [P, 2])
        veps = sb("veps", [P, 1])
        lnv = sb("lnv", [P, 1])
        rs0 = sb("rs0", [P, 1])
        rs1 = sb("rs1", [P, 1])
        rs2 = sb("rs2", [P, 1])
        rstd = sb("rstd", [P, 1])

        acc = pb("acc")
        tr = pb("tr")
        hp = [pb(f"hp{i}") for i in range(3)]
        rowb = pb("rowb")
        pw = ctx.enter_context(nc.psum_tensor("pw", [P, KH, 512], F32))
        cnt_ps = pw[:, 0, 0:R]
        inv_ps = pw[:, 1, 0:J * R].rearrange("p (j r) -> p j r", j=J)

        names = """ld_nat_a ld_nat_b ld_nxt ld_x ld_w ld_par nat_zero ground made nat_conv nat_join col_tr col_out
                   tb_cmp tb_cols tb_rows tb_table tab_ready
                   wm_zero key_masked key_row_ready w_ready w_cols w_dup w_last w_hot w_mm w_upd
                   xcur_ready x_tr xT_ready x_mm
                   cnt_iota cnt_cols cnt_S cnt_mm cnt_max inv_ready inv_zero dst_masked dst_row_ready ST_ready
                   inv_mm inv_prod inv_sum inv_upd
                   iota_ready gd_copied S_ready agg_mm idx_copied tiles_landed passed
                   y_part y_ready n_stats n_mv n_veps n_ln n_rs0 n_newton n_norm n_gamma n_beta n_min n_exp n_elu
                   xn_ready xn_stored xn_tr xnT_ready h_mm h_out h_stored
                   x1_saved x1_back f_sum f_stats f_mv f_veps f_ln f_rs0 f_newton f_norm out_stored""".split()
        s = {n: sem(n) for n in names}
        landed = [sem(f"landed{k}") for k in range(SLOTS)]

        block = ctx.enter_context(nc.Block())

        MAXS = NT * NG * L

        def entry(eng, col, lo, hi):
            return eng.value_load(tab[0:1, bass.ds(col, 1)], min_val=lo, max_val=hi)

        def tile_bounds(eng, t):
            return entry(eng, t + T_LO, 0, NG - 1), entry(eng, t + T_HI, 1, NG), entry(eng, t + T_SB, 0, MAXS)

        @block.sync
        def _(sp):
            sp.wait_ge(s["nat_zero"], 5)
            full, rest = (NG - 1) * GE, E - (NG - 1) * GE
            for a, b in ((dst, nat_dst_i), (src, nat_src_i), (etype, nat_typ_i), (eweight, nat_w)):
                sp.dma_start(b[0:NG - 1, :], a[0:full].rearrange("(g e) -> g e", e=GE)).then_inc(s["ld_nat_a"], 16)
                sp.dma_start(b[NG - 1:NG, 0:rest], a[full:E].rearrange("(g e) -> g e", e=rest)).then_inc(s["ld_nat_b"], 16)
            sp.dma_start(nxt_i[0:NG - 2, :], dst[GE:full].rearrange("(g e) -> g e", e=GE)[:, 0:1],
                         allow_slow_non_contiguous=True).then_inc(s["ld_nxt"], 16)
            sp.dma_start(nxt_i[NG - 2:NG - 1, :], dst[full:full + 1].rearrange("(g e) -> g e", e=1)).then_inc(s["ld_nxt"], 16)
            sp.dma_start(X[:, 0:NT - 1, :], x[0:(NT - 1) * P, :].rearrange("(t p) d -> p t d", p=P)).then_inc(s["ld_x"], 16)
            sp.dma_start(X[0:N - (NT - 1) * P, NT - 1, :], x[(NT - 1) * P:N, :]).then_inc(s["ld_x"], 16)
            for l in range(L):
                for k in range(KH):
                    for r in range(R):
                        sp.dma_start(wts[:, l, k, r * D:(r + 1) * D], weights[l, r, k * P:(k + 1) * P, :]).then_inc(s["ld_w"], 16)
                    sp.dma_start(wts[:, l, k, R * D:NB], roots[l, k * P:(k + 1) * P, :]).then_inc(s["ld_w"], 16)
            for a, b in ((biases, bias_b), (gammas, gamma_b), (betas, beta_b)):
                sp.dma_start(b[:], a.rearrange("(o l) d -> o l d", o=1).to_broadcast([P, L, D])).then_inc(s["ld_par"], 16)

            sp.wait_ge(s["tab_ready"], 1)
            passes = entry(sp, T_P, 1, NT)
            with sp.Fori(0, L) as l:
                lc = entry(sp, l + T_LC, 0, L * NT * CYC)
                with sp.Fori(0, passes) as p:
                    with sp.Fori(0, CYC) as c:
                        for k in range(SLOTS):
                            sp.wait_ge(landed[k], (lc + p * CYC + c + 1) * 16)
                            sp.sem_inc(s["tiles_landed"], 1)

        @block.gpsimd
        def _(pool):
            pool.memset(nat_dst_i, NP).then_inc(s["nat_zero"], 1)
            pool.memset(nat_src_i, 0).then_inc(s["nat_zero"], 1)
            pool.memset(nat_typ_i, 0).then_inc(s["nat_zero"], 1)
            pool.memset(nat_w, 0.0).then_inc(s["nat_zero"], 1)
            pool.memset(X[:, NT - 1, :], 0.0)
            pool.memset(nxt_i[:], NP).then_inc(s["nat_zero"], 1)
            pool.memset(ident[:], 0.0)
            pool.memset(ones[:], 1.0)
            pool.memset(later, 1.0)
            pool.memset(tri[:], 0.0)
            pool.memset(zeros[:], 0.0)
            pool.iota(iota[:], [[1, D]], base=0, channel_multiplier=0, allow_small_or_imprecise_dtypes=True)
            pool.iota(pnode[:], [[P, NT]], base=0, channel_multiplier=1, allow_small_or_imprecise_dtypes=True)
            pool.iota(tbase[:], [[P, NT]], base=0, channel_multiplier=0, allow_small_or_imprecise_dtypes=True)
            pool.iota(grow[:], [[1, NG]], base=1 - RG, channel_multiplier=0, allow_small_or_imprecise_dtypes=True).then_inc(s["ground"], 1)
            pool.wait_ge(s["ground"], 1)
            pool.affine_select(out=ident[:], in_=ident[:], compare_op=ALU.not_equal, fill=1.0, base=0,
                               pattern=[[-1, P]], channel_multiplier=1)
            pool.affine_select(out=later, in_=later, compare_op=ALU.is_gt, fill=0.0, base=0,
                               pattern=[[1, GE]], channel_multiplier=-1)
            pool.affine_select(out=tri[:], in_=tri[:], compare_op=ALU.is_ge, fill=1.0, base=0,
                               pattern=[[-1, NT]], channel_multiplier=1).then_inc(s["made"], 1)

            pool.wait_ge(s["w_mm"], 1)
            pool.wait_ge(s["w_ready"], 1)
            passes = entry(pool, T_P, 1, NT)
            def gathers(l, h_gather):
                pool.wait_ge(s["h_stored"], (l + 1) * (16 * NT))
                pool.sem_inc(s["passed"], 1)
                lm = entry(pool, l + T_LM, 0, MAXS)
                lc = entry(pool, l + T_LC, 0, L * NT * CYC)
                with pool.Fori(0, passes) as p:
                    with pool.Fori(0, CYC) as c:
                        for g in range(RG):
                            rel = entry(pool, c * RG + (T_REL + g), 1, MAXS * J)
                            pool.wait_ge(s["agg_mm"], (lm + p * NG) * J + rel)
                            pool.sem_inc(s["passed"], 1)
                            pool.tensor_copy(ixb[:, g * J:(g + 1) * J], idx[:, bass.ds(c * SLOTS + g * J, J)]).then_inc(s["idx_copied"], 1)
                            pool.wait_ge(s["idx_copied"], (lc + p * CYC + c) * RG + (g + 1))
                            pool.sem_inc(s["passed"], 1)
                            for j in range(J):
                                k = g * J + j
                                pool.indirect_dma_start(ring[:, k, :], None, h_gather,
                                                        bass.IndirectOffsetOnAxis(ap=ixb[:, k:k + 1], axis=0)).then_inc(landed[k], 16)

            with pool.Fori(0, L // 2) as two:
                for half in range(2):
                    gathers(two * 2 + half, h_rows[half].rearrange("n (r d) -> (n r) d", r=R))

        @block.tensor
        def _(pe):
            pe.sem_inc(s["agg_mm"], BIAS)
            pe.sem_inc(s["cnt_mm"], J)
            pe.sem_inc(s["cnt_S"], J)
            pe.sem_inc(s["S_ready"], J)
            pe.wait_ge(s["made"], 1)

            pe.wait_ge(s["nat_join"], 2)
            for a, arr in enumerate((nat_dst[:], nat_src, nat_key, nat_w, nat_idx, nat_typ)):
                bank = (tr, rowb)[a % 2]
                if a >= 2:
                    pe.wait_ge(s["col_out"], a - 1)
                for j in range(J):
                    m = nc.tensor.transpose(bank[:, j * P:j * P + NG], arr[:, j * P:(j + 1) * P], ident[0:NG, 0:NG])
                m.then_inc(s["col_tr"], 1)

            pe.wait_ge(s["tb_cmp"], 6)
            nc.tensor.matmul(acc[0:NT, 0:1], cmp[:, 0:NT], ones[0:NG, 0:1], start=True, stop=True)
            nc.tensor.matmul(acc[0:NT, 8:9], cmp[:, 32:32 + NT], ones[0:NG, 0:1], start=True, stop=True)
            nc.tensor.matmul(acc[0:NT, 16:17], ones[0:NG, 0:NT], bad[:, 2:3], start=True, stop=True).then_inc(s["tb_rows"], 1)
            pe.wait_ge(s["tb_cols"], 12)
            nc.tensor.matmul(acc[0:1, 32:32 + NT], colv[:, 6:7], ident[0:NT, 0:NT], start=True, stop=True)
            nc.tensor.matmul(acc[0:1, 64:64 + NT], colv[:, 8:9], ident[0:NT, 0:NT], start=True, stop=True)
            nc.tensor.matmul(acc[0:1, 96:96 + NT], colv[:, 9:10], tri[0:NT, :], start=True, stop=False)
            nc.tensor.matmul(acc[0:1, 96:96 + NT], colv[:, 10:11], ident[0:NT, 0:NT], start=False, stop=True)
            nc.tensor.matmul(acc[0:1, 128:129], colv[:, 9:10], ones[0:NT, 0:1], start=True, stop=True)
            nc.tensor.matmul(acc[0:1, 132:133], colv[0:1, 3:4], ones[0:1, 0:1], start=True, stop=True)
            nc.tensor.matmul(acc[0:1, 160:160 + NG], ones[0:NT, 0:1], relx[:], start=True, stop=True).then_inc(s["tb_rows"], 1)

            pe.wait_ge(s["tab_ready"], 1)
            for t in range(KH):
                lo_t, end_t, sb_t = tile_bounds(pe, t)
                with pe.Fori(lo_t, end_t) as g:
                    w = sb_t + g
                    pe.wait_ge(s["key_masked"], w + 1)
                    nc.tensor.matmul(rowb[:], ones[0:NG, :], key_row, start=True, stop=True).then_inc(s["key_row_ready"], 1)
                    for j in range(J):
                        pe.wait_ge(s["w_hot"], w * J + (j + 1))
                        for k in range(KH):
                            m = nc.tensor.matmul(pw[:, k, 0:2 * P], OS[:, j, k * P:(k + 1) * P],
                                                 OD[:, j, :, :].rearrange("p c n -> p (c n)"), start=j == 0, stop=j == J - 1)
                    m.then_inc(s["w_mm"], 1)

            def node_products(e, layer, first=False):
                pe.wait_ge(s["xn_ready"], e + 1)
                for k in range(KH):
                    m = nc.tensor.transpose(tr[:, k * P:(k + 1) * P], xn[:, k * P:(k + 1) * P], ident[:])
                m.then_inc(s["xn_tr"], 1)
                if not first:
                    pe.wait_ge(s["h_out"], e * 3)
                pe.wait_ge(s["xnT_ready"], e + 1)
                for b, (c0, c1) in enumerate(((0, 512), (512, 1024), (1024, NB))):
                    for k in range(KH):
                        rhs = wts[:, bass.ds(layer, 1), k, c0:c1].rearrange("p a c -> p (a c)")
                        m = nc.tensor.matmul(hp[b][:, 0:c1 - c0], xnT[:, k, :], rhs, start=k == 0, stop=k == KH - 1)
                    m.then_inc(s["h_mm"], 1)

            def first_product(t, first=False):
                pe.wait_ge(s["xcur_ready"], t + 1)
                for k in range(KH):
                    m = nc.tensor.transpose(tr[:, D + k * P:D + (k + 1) * P], xcur[:, k * P:(k + 1) * P], ident[:])
                m.then_inc(s["x_tr"], 1)
                if not first:
                    pe.wait_ge(s["y_ready"], t)
                pe.wait_ge(s["xT_ready"], t + 1)
                for k in range(KH):
                    m = nc.tensor.matmul(acc[:, 0:D], xT[:, k, :], Wm[:, k, :], start=k == 0, stop=k == KH - 1)
                m.then_inc(s["x_mm"], 1)

            pe.wait_ge(s["w_ready"], 1)
            pe.wait_ge(s["ld_w"], 16 * L * KH * (R + 1))
            first_product(0, first=True)
            first_product(1)
            node_products(0, 0, first=True)
            with pe.Fori(2, NT) as t:
                first_product(t)
                node_products(t - 1, 0)
            node_products(NT - 1, 0)

            pe.wait_ge(s["inv_zero"], 1)
            with pe.Fori(0, NT) as t:
                lo_t, end_t, sb_t = tile_bounds(pe, t)
                nc.tensor.matmul(cnt_ps, zeros[:, 0:P], zeros[:, 0:R], start=True, stop=True)
                with pe.Fori(lo_t, end_t) as g:
                    for j in range(J):
                        pe.wait_ge(s["cnt_S"], (sb_t + g) * J + (J + j + 1))
                        nc.tensor.matmul(cnt_ps, S[:, j, :], toh[:, bass.ds(g, 1), j, :].rearrange("p a r -> p (a r)"),
                                         start=False, stop=True, skip_group_check=True).then_inc(s["cnt_mm"], 1)
                pe.wait_ge(s["inv_ready"], t + 1)
                pe.sem_inc(s["passed"], 1)
                with pe.Fori(lo_t, end_t) as g:
                    w = sb_t + g
                    pe.wait_ge(s["dst_masked"], w + 1)
                    nc.tensor.matmul(rowb[:], ones[0:NG, :], dst_row[:], start=True, stop=True).then_inc(s["dst_row_ready"], 1)
                    pe.wait_ge(s["ST_ready"], w + 1)
                    for j in range(J):
                        m = nc.tensor.matmul(inv_ps[:, j, :], ST[:, j * P:(j + 1) * P], invd[:], start=True, stop=True)
                    m.then_inc(s["inv_mm"], 1)

            def aggregate(l, t, lm, lg):
                lo_t, end_t, sb_t = tile_bounds(pe, t)
                gb_t = entry(pe, t + T_GB, 0, MAXS * J)
                pe.wait_ge(s["y_part"], l * NT + (t + NT))
                nc.tensor.matmul(acc[:, 0:D], zeros[:, 0:P], zeros[:], start=True, stop=True)
                with pe.Fori(lo_t, end_t) as g:
                    for j in range(J):
                        pe.wait_ge(s["S_ready"], (lm + sb_t + g) * J + (J + j + 1))
                        pe.wait_ge(s["tiles_landed"], lg + gb_t + g * J + (j + 1))
                        nc.tensor.matmul(acc[:, 0:D], S[:, j, :],
                                         ring[:, bass.ds(g % RG * J + j, 1), :].rearrange("p a d -> p (a d)"),
                                         start=False, stop=True, skip_group_check=True).then_inc(s["agg_mm"], 1)

            with pe.Fori(0, L - 1) as l:
                lm = entry(pe, l + T_LM, 0, MAXS)
                lg = entry(pe, l + T_LG, 0, MAXS * J)
                aggregate(l, 0, lm, lg)
                with pe.Fori(1, NT) as t:
                    aggregate(l, t, lm, lg)
                    node_products(l * NT + (t + NT - 1), l + 1)
                node_products(l * NT + (2 * NT - 1), l + 1)
            lm = entry(pe, T_LM + L - 1, 0, MAXS)
            lg = entry(pe, T_LG + L - 1, 0, MAXS * J)
            with pe.Fori(0, NT) as t:
                aggregate(L - 1, t, lm, lg)

        @block.scalar
        def _(act):
            def transposed(e, first=False):
                act.wait_ge(s["xn_tr"], e + 1)
                if not first:
                    act.wait_ge(s["h_mm"], e * 3)
                nc.scalar.activation(xnT[:].rearrange("p k n -> p (k n)"), tr[:, 0:D], ACT.Copy).then_inc(s["xnT_ready"], 1)

            def products_out(e, t, half, first=False):
                act.wait_ge(s["h_mm"], e * 3 + 1)
                if not first:
                    act.wait_ge(s["h_stored"], e * 16)
                nc.scalar.activation(hst[:, 0:512], hp[0][:], ACT.Copy).then_inc(s["h_out"], 1)
                act.wait_ge(s["h_mm"], e * 3 + 2)
                nc.scalar.activation(hst[:, 512:1024], hp[1][:], ACT.Copy).then_inc(s["h_out"], 1)
                act.wait_ge(s["h_mm"], e * 3 + 3)
                act.sem_inc(s["passed"], 1)
                nc.scalar.activation(base[:, bass.ds(t, 1), :].rearrange("p a d -> p (a d)"), hp[2][:, 0:D],
                                     ACT.Copy).then_inc(s["h_out"], 1)
                act.wait_ge(s["h_out"], e * 3 + 2)
                act.dma_start(h_rows[half][bass.ds(t * P, P), :], hst[:]).then_inc(s["h_stored"], 16)

            def root(e, pre):
                act.wait_ge(s[pre + "veps"], e + 1)
                nc.scalar.activation(lnv[:], veps[:], ACT.Ln).then_inc(s[pre + "ln"], 1)
                act.wait_ge(s[pre + "ln"], e + 1)
                nc.scalar.activation(rs0[:], lnv[:], ACT.Exp, scale=-0.5).then_inc(s[pre + "rs0"], 1)

            def store_xn(e, t):
                act.wait_ge(s["xn_ready"], e + 1)
                act.sem_inc(s["passed"], 1)
                nc.scalar.activation(X[:, bass.ds(t, 1), :].rearrange("p a d -> p (a d)"), xn[:], ACT.Copy).then_inc(s["xn_stored"], 1)

            def current_x(t, first=False):
                if not first:
                    act.wait_ge(s["x_tr"], t)
                    act.sem_inc(s["passed"], 1)
                nc.scalar.activation(xcur[:], X[:, bass.ds(t, 1), :].rearrange("p a d -> p (a d)"), ACT.Copy).then_inc(s["xcur_ready"], 1)

            def x_transposed(t, first=False):
                act.wait_ge(s["x_tr"], t + 1)
                if not first:
                    act.wait_ge(s["x_mm"], t)
                nc.scalar.activation(xT[:].rearrange("p k n -> p (k n)"), tr[:, D:2 * D], ACT.Copy).then_inc(s["xT_ready"], 1)

            act.wait_ge(s["ld_x"], 32)
            act.wait_ge(s["w_ready"], 1)
            current_x(0, first=True)
            x_transposed(0, first=True)
            current_x(1)
            root(0, "n_")
            store_xn(0, 0)
            x_transposed(1)
            transposed(0, first=True)
            current_x(2)
            root(1, "n_")
            store_xn(1, 1)
            products_out(0, 0, 0, first=True)
            with act.Fori(2, NT - 1) as t:
                x_transposed(t)
                transposed(t - 1)
                current_x(t + 1)
                root(t, "n_")
                store_xn(t, t)
                products_out(t - 1, t - 1, 0)
            t = NT - 1
            x_transposed(t)
            transposed(t - 1)
            root(t, "n_")
            store_xn(t, t)
            products_out(t - 1, t - 1, 0)
            transposed(t)
            products_out(t, t, 0)

            act.wait_ge(s["xn_stored"], NT)
            act.dma_start(x1_rows, X[:].rearrange("p t d -> p (t d)")).then_inc(s["x1_saved"], 16)
            act.wait_ge(s["x1_saved"], 16)
            act.sem_inc(s["passed"], 1)

            def elu_exp(el):
                act.wait_ge(s["n_min"], el + 1)
                nc.scalar.activation(ze[:], zm[:], ACT.Exp).then_inc(s["n_exp"], 1)

            for l in range(L - 1):
                half = (l + 1) % 2
                root(l * NT + NT, "n_")
                elu_exp(l * NT)
                store_xn(l * NT + NT, 0)
                with act.Fori(1, NT) as t:
                    e = l * NT + (t + NT)
                    transposed(l * NT + (t + NT - 1))
                    root(e, "n_")
                    elu_exp(l * NT + t)
                    store_xn(e, t)
                    products_out(l * NT + (t + NT - 1), t - 1, half)
                transposed(l * NT + (2 * NT - 1))
                products_out(l * NT + (2 * NT - 1), NT - 1, half)

            act.wait_ge(s["h_mm"], L * NT * 3)
            act.dma_start(x1.rearrange("p t d -> p (t d)"), x1_rows).then_inc(s["x1_back"], 16)

            def last_layer(t):
                root(t + L * NT, "n_")
                elu_exp(t + (L - 1) * NT)
                root(t, "f_")

            with act.Fori(0, NT - 1) as t:
                last_layer(t)
                act.wait_ge(s["f_norm"], t + 1)
                act.dma_start(out[bass.ds(t * P, P), :], yo[:]).then_inc(s["out_stored"], 16)
            last_layer(NT - 1)
            act.wait_ge(s["f_norm"], NT)
            act.dma_start(out[(NT - 1) * P:N, :], yo[0:N - (NT - 1) * P, :]).then_inc(s["out_stored"], 16)
            act.wait_ge(s["out_stored"], 16 * NT)

        @block.vector
        def _(dve):
            v = nc.vector
            dve.wait_ge(s["ld_nat_a"], 16 * 4)
            dve.wait_ge(s["ld_nat_b"], 16 * 4)
            v.tensor_copy(nat_dst[:], nat_dst_i)
            v.tensor_copy(nat_src, nat_src_i)
            v.tensor_copy(nat_typ, nat_typ_i).then_inc(s["nat_conv"], 1)
            dve.wait_ge(s["nat_conv"], 1)
            v.scalar_tensor_tensor(out=nat_key, in0=nat_src, scalar=float(KEY), in1=nat_dst[:], op0=ALU.mult, op1=ALU.add).then_inc(s["nat_join"], 1)
            v.scalar_tensor_tensor(out=nat_idx, in0=nat_src, scalar=float(R), in1=nat_typ, op0=ALU.mult, op1=ALU.add).then_inc(s["nat_join"], 1)

            dve.wait_ge(s["made"], 1)
            dve.wait_ge(s["ld_nxt"], 32)
            v.tensor_scalar(cmp[:, 0:NT], tbase[0:NG, :], nat_dst[:, 0:1], float(-P), ALU.subtract, ALU.is_gt).then_inc(s["tb_cmp"], 1)
            v.tensor_scalar(cmp[:, 32:32 + NT], tbase[0:NG, :], nat_dst[:, GE - 1:GE], 0.0, ALU.subtract, ALU.is_gt).then_inc(s["tb_cmp"], 1)
            v.tensor_tensor(junk[0:NG, 0:GE - 1], nat_dst[:, 1:GE], nat_dst[:, 0:GE - 1], ALU.is_lt)
            v.tensor_copy(nxt[:], nxt_i[:]).then_inc(s["tb_cmp"], 1)
            dve.wait_ge(s["tb_cmp"], 3)
            v.tensor_reduce(bad[:, 0:1], junk[0:NG, 0:GE - 1], AX.X, ALU.max).then_inc(s["tb_cmp"], 1)
            v.tensor_tensor(bad[:, 1:2], nxt[:], nat_dst[:, GE - 1:GE], ALU.is_lt).then_inc(s["tb_cmp"], 1)
            dve.wait_ge(s["tb_cmp"], 5)
            v.tensor_tensor(bad[:, 2:3], bad[:, 0:1], bad[:, 1:2], ALU.max).then_inc(s["tb_cmp"], 1)

            dup_at = [sum(GE - k * P for k in range(j)) for j in range(J + 1)]

            def columns(a, out_ap, bank):
                dve.wait_ge(s["col_tr"], a + 1)
                return v.tensor_scalar(out_ap, bank[:].rearrange("p (j g) -> p j g", j=J)[:, :, 0:NG].rearrange("p j g -> p g j"),
                                       0.0, None, ALU.add)
            for a in range(4):
                columns(a, ecol[:, :, a, :], (tr, rowb)[a % 2]).then_inc(s["col_out"], 1)
            columns(4, idx[:].rearrange("p (g j) -> p g j", j=J), tr).then_inc(s["col_out"], 1)
            dve.wait_ge(s["col_tr"], 6)
            for r in range(R):
                v.tensor_scalar(toh[:, :, :, r], rowb[:].rearrange("p (j g) -> p j g", j=J)[:, :, 0:NG].rearrange("p j g -> p g j"),
                                float(r), None, ALU.is_equal)

            c = lambda n: colv[:, n:n + 1]
            step = [0]

            def col(ins):
                step[0] += 1
                ins.then_inc(s["tb_cols"], 1)
                dve.wait_ge(s["tb_cols"], step[0])
            dve.wait_ge(s["tb_rows"], 1)
            col(v.tensor_scalar(c(3), acc[0:NT, 16:17], 1.0, None, ALU.min))
            col(v.tensor_scalar(c(4), c(3), -1.0, 1.0, ALU.mult, ALU.add))
            col(v.tensor_scalar(c(1), acc[0:NT, 0:1], 1.0, None, ALU.max))
            col(v.tensor_scalar(c(5), c(1), 1.0, None, ALU.subtract))
            col(v.tensor_tensor(c(0), acc[0:NT, 8:9], c(5), ALU.min))
            col(v.tensor_tensor(c(6), c(0), c(4), ALU.mult))
            col(v.tensor_tensor(c(7), c(1), c(4), ALU.mult))
            col(v.scalar_tensor_tensor(out=c(8), in0=c(3), scalar=float(NG), in1=c(7), op0=ALU.mult, op1=ALU.add))
            col(v.tensor_tensor(c(9), c(8), c(6), ALU.subtract))
            col(v.tensor_scalar(c(10), c(6), -1.0, None, ALU.mult))
            col(v.tensor_scalar(relw[:], grow[0:NT, :], c(8), c(6), ALU.min, ALU.subtract))
            col(v.tensor_scalar(relx[:], relw[:], 0.0, None, ALU.max))

            r_ = lambda n: rowv[:, n:n + 1]
            count = [0]

            def row(ins):
                count[0] += 1
                ins.then_inc(s["tb_table"], 1)
                dve.wait_ge(s["tb_table"], count[0])
            dve.wait_ge(s["tb_rows"], 2)
            row(v.memset(tabf[:], 0.0))
            row(v.tensor_scalar(r_(0), acc[0:1, 128:129], 0.0, None, ALU.add))
            row(v.tensor_scalar(r_(1), acc[0:1, 132:133], 0.0, None, ALU.add))
            row(v.tensor_scalar(r_(2), r_(1), -1.0, 1.0, ALU.mult, ALU.add))
            row(v.tensor_scalar(r_(3), r_(1), float(NT - 1), 1.0, ALU.mult, ALU.add))
            v.tensor_scalar(tabf[:, T_P:T_P + 1], r_(3), 0.0, None, ALU.add)
            v.tensor_scalar(tabf[:, T_LO:T_LO + NT], acc[0:1, 32:32 + NT], 0.0, None, ALU.add)
            v.tensor_scalar(tabf[:, T_HI:T_HI + NT], acc[0:1, 64:64 + NT], 0.0, None, ALU.add)
            v.tensor_scalar(tabf[:, T_SB:T_SB + NT], acc[0:1, 96:96 + NT], 0.0, None, ALU.add)
            v.tensor_scalar(tabf[:, T_GB:T_GB + NT], tbase[0:1, :], r_(1), float(NG * J) / P, ALU.mult, ALU.mult)
            v.tensor_scalar(tabf[:, T_LM:T_LM + L], iota[0:1, 0:L], r_(0), None, ALU.mult)
            v.tensor_scalar(tabf[:, T_LG:T_LG + L], iota[0:1, 0:L], r_(3), float(NG * J), ALU.mult, ALU.mult)
            v.tensor_scalar(tabf[:, T_LC:T_LC + L], iota[0:1, 0:L], r_(3), float(CYC), ALU.mult, ALU.mult)
            row(v.tensor_scalar(relr[:], acc[0:1, 160:160 + NG], r_(2), None, ALU.mult))
            row(v.scalar_tensor_tensor(out=relr2[:], in0=grow[0:1, :], scalar=r_(1), in1=relr[:], op0=ALU.mult, op1=ALU.add))
            row(v.tensor_scalar(tabf[:, T_REL:T_END], relr2[:], float(J), float(BIAS), ALU.mult, ALU.add))
            v.memset(Wm[:], 0.0).then_inc(s["wm_zero"], 1)
            v.tensor_copy(tab[:], tabf[:]).then_inc(s["tab_ready"], 1)
            dve.wait_ge(s["tab_ready"], 1)
            dve.wait_ge(s["wm_zero"], 1)

            for t in range(KH):
                lo_t, end_t, sb_t = tile_bounds(dve, t)
                Wt = Wm[:, :, t * P:(t + 1) * P]
                with dve.Fori(lo_t, end_t) as g:
                    w = sb_t + g
                    v.tensor_scalar(key_row, nat_key, ident[0:NG, bass.ds(g, 1)], None, ALU.mult).then_inc(s["key_masked"], 1)
                    v.tensor_copy(gcol[:], ecol[:, bass.ds(g, 1), :, :].rearrange("p a c j -> p (a c) j")).then_inc(s["w_cols"], 1)
                    dve.wait_ge(s["w_cols"], w + 1)
                    dve.wait_ge(s["key_row_ready"], w + 1)
                    for j in range(J):
                        v.scalar_tensor_tensor(out=dupw[:, dup_at[j]:dup_at[j + 1]], in0=rowb[:, j * P:GE], scalar=gcol[:, 2, j:j + 1],
                                               in1=later[:, 0:GE - j * P], op0=ALU.is_equal, op1=ALU.mult,
                                               accum_out=dup[:, j:j + 1]).then_inc(s["w_dup"], 1)
                    dve.wait_ge(s["w_dup"], w * J + J)
                    v.scalar_tensor_tensor(out=wlast[:], in0=dup[:], scalar=0.0, in1=gcol[:, 3, :], op0=ALU.is_equal,
                                           op1=ALU.mult).then_inc(s["w_last"], 1)
                    dve.wait_ge(s["w_last"], w + 1)
                    for j in range(J):
                        v.tensor_scalar(OS[:, j, :], iota[:], gcol[:, 1, j:j + 1], None, ALU.is_equal)
                        v.tensor_scalar(OD[:, j, 0, :], iota[:, t * P:(t + 1) * P], gcol[:, 0, j:j + 1], None, ALU.is_equal)
                        v.tensor_scalar(OD[:, j, 1, :], iota[:, t * P:(t + 1) * P], gcol[:, 0, j:j + 1], wlast[:, j:j + 1],
                                        ALU.is_equal, ALU.mult).then_inc(s["w_hot"], 1)
                    dve.wait_ge(s["w_mm"], w + 1)
                    v.scalar_tensor_tensor(out=Wt, in0=pw[:, :, 0:P], scalar=0.0, in1=Wt, op0=ALU.is_equal,
                                           op1=ALU.mult).then_inc(s["w_upd"], 1)
                    dve.wait_ge(s["w_upd"], w * 2 + 1)
                    v.tensor_tensor(Wt, Wt, pw[:, :, P:2 * P], ALU.add).then_inc(s["w_upd"], 1)
                    dve.wait_ge(s["w_upd"], w * 2 + 2)
            v.memset(ecol[:, :, 1, :], 0.0).then_inc(s["inv_zero"], 1)
            dve.sem_inc(s["w_ready"], 1)

            def normalise(e, pre, y_in, out_ap):
                v.bn_stats(st6[:], y_in).then_inc(s[pre + "stats"], 1)
                dve.wait_ge(s[pre + "stats"], e + 1)
                dve.sem_inc(s["passed"], 1)
                v.bn_aggr(mv[:], st6[:]).then_inc(s[pre + "mv"], 1)
                dve.wait_ge(s[pre + "mv"], e + 1)
                v.tensor_scalar(veps[:], mv[:, 1:2], EPS, None, ALU.add).then_inc(s[pre + "veps"], 1)
                dve.wait_ge(s[pre + "rs0"], e + 1)
                v.scalar_tensor_tensor(out=rs1[:], in0=rs0[:], scalar=rs0[:], in1=veps[:], op0=ALU.mult, op1=ALU.mult).then_inc(s[pre + "newton"], 1)
                dve.wait_ge(s[pre + "newton"], e * 3 + 1)
                v.tensor_scalar(rs2[:], rs1[:], -0.5, 1.5, ALU.mult, ALU.add).then_inc(s[pre + "newton"], 1)
                dve.wait_ge(s[pre + "newton"], e * 3 + 2)
                v.tensor_tensor(rstd[:], rs2[:], rs0[:], ALU.mult).then_inc(s[pre + "newton"], 1)
                dve.wait_ge(s[pre + "newton"], e * 3 + 3)
                return v.tensor_scalar(out_ap, y_in, mv[:, 0:1], rstd[:], ALU.subtract, ALU.mult)

            def first_norm(t, first=False):
                dve.wait_ge(s["x_mm"], t + 1)
                v.tensor_tensor(y[:], acc[:, 0:D], X[:, bass.ds(t, 1), :].rearrange("p a d -> p (a d)"), ALU.add).then_inc(s["y_ready"], 1)
                dve.wait_ge(s["y_ready"], t + 1)
                if not first:
                    dve.wait_ge(s["xn_tr"], t)
                    dve.wait_ge(s["xn_stored"], t)
                normalise(t, "n_", y[:], xn[:]).then_inc(s["xn_ready"], 1)
            first_norm(0, first=True)
            with dve.Fori(1, NT) as t:
                first_norm(t)

            dve.wait_ge(s["inv_zero"], 1)
            dve.wait_ge(s["y_ready"], NT)
            dve.sem_inc(s["y_part"], NT)
            with dve.Fori(0, NT) as t:
                lo_t, end_t, sb_t = tile_bounds(dve, t)
                dve.wait_ge(s["cnt_S"], (sb_t + lo_t) * J + J)
                v.tensor_scalar(iota_t[:], iota[:, 0:P], tbase[:, bass.ds(t, 1)], None, ALU.add).then_inc(s["cnt_iota"], 1)
                dve.wait_ge(s["cnt_iota"], t + 1)
                dve.sem_inc(s["passed"], 1)
                with dve.Fori(lo_t, end_t) as g:
                    w = sb_t + g
                    dve.wait_ge(s["cnt_S"], w * J + J)
                    dve.sem_inc(s["passed"], 1)
                    v.tensor_copy(gdi[:, 0, :], ecol[:, bass.ds(g, 1), 0, :].rearrange("p a j -> p (a j)")).then_inc(s["cnt_cols"], 1)
                    dve.wait_ge(s["cnt_cols"], w + 1)
                    for j in range(J):
                        dve.wait_ge(s["cnt_mm"], w * J + (j + 1))
                        v.tensor_scalar(S[:, j, :], iota_t[:], gdi[:, 0, j:j + 1], None, ALU.is_equal).then_inc(s["cnt_S"], 1)
                dve.wait_ge(s["cnt_mm"], (sb_t + end_t) * J + J)
                v.tensor_scalar(cntm[:], cnt_ps, 1.0, None, ALU.max).then_inc(s["cnt_max"], 1)
                dve.wait_ge(s["cnt_max"], t + 1)
                v.reciprocal(invd[:], cntm[:]).then_inc(s["inv_ready"], 1)
                with dve.Fori(lo_t, end_t) as g:
                    w = sb_t + g
                    v.tensor_scalar(dst_row[:], nat_dst[:], ident[0:NG, bass.ds(g, 1)], None, ALU.mult).then_inc(s["dst_masked"], 1)
                    dve.wait_ge(s["dst_row_ready"], w + 1)
                    v.tensor_scalar(ST[:], rowb[:], pnode[:, bass.ds(t, 1)], None, ALU.is_equal).then_inc(s["ST_ready"], 1)
                    dve.wait_ge(s["inv_mm"], w + 1)
                    v.tensor_tensor(prod[:], inv_ps, toh[:, bass.ds(g, 1), :, :].rearrange("p a j r -> p (a j) r"), ALU.mult).then_inc(s["inv_prod"], 1)
                    dve.wait_ge(s["inv_prod"], w + 1)
                    v.tensor_reduce(psum4[:], prod[:], AX.X, ALU.add).then_inc(s["inv_sum"], 1)
                    dve.wait_ge(s["inv_sum"], w + 1)
                    einv = ecol[:, bass.ds(g, 1), 1, :].rearrange("p a j -> p (a j)")
                    v.tensor_tensor(einv, einv, psum4[:], ALU.add).then_inc(s["inv_upd"], 1)
                    dve.wait_ge(s["inv_upd"], w + 1)

            dve.wait_ge(s["ld_par"], 48)

            def weigh(l, t, lm):
                lo_t, end_t, sb_t = tile_bounds(dve, t)
                dve.wait_ge(s["S_ready"], (lm + sb_t + lo_t) * J + J)
                v.tensor_scalar(iota_t[:], iota[:, 0:P], tbase[:, bass.ds(t, 1)], None, ALU.add).then_inc(s["iota_ready"], 1)
                dve.wait_ge(s["iota_ready"], l * NT + (t + 1))
                dve.sem_inc(s["passed"], 1)
                with dve.Fori(lo_t, end_t) as g:
                    w = lm + sb_t + g
                    dve.wait_ge(s["S_ready"], w * J + J)
                    dve.sem_inc(s["passed"], 1)
                    v.tensor_copy(gdi[:], ecol[:, bass.ds(g, 1), 0:2, :].rearrange("p a c j -> p (a c) j")).then_inc(s["gd_copied"], 1)
                    dve.wait_ge(s["gd_copied"], w + 1)
                    for j in range(J):
                        dve.wait_ge(s["agg_mm"], w * J + (j + 1 + BIAS - J))
                        v.tensor_scalar(S[:, j, :], iota_t[:], gdi[:, 0, j:j + 1], gdi[:, 1, j:j + 1],
                                        ALU.is_equal, ALU.mult).then_inc(s["S_ready"], 1)
                return lm + sb_t + end_t

            def layer_norm_elu(l, t, steps, out_ap, out_sem):
                def of(a):
                    return a[:, bass.ds(l, 1), :].rearrange("p a d -> p (a d)")
                e, el = l * NT + (t + NT), l * NT + t
                xt = X[:, bass.ds(t, 1), :].rearrange("p a d -> p (a d)")
                bt = base[:, bass.ds(t, 1), :].rearrange("p a d -> p (a d)")
                dve.wait_ge(s["agg_mm"], steps * J + BIAS)
                v.tensor_tensor(ysum[:], acc[:, 0:D], bt, ALU.add).then_inc(s["y_part"], 1)
                dve.wait_ge(s["y_part"], e + 1)
                v.tensor_tensor(y[:], ysum[:], of(bias_b), ALU.add).then_inc(s["y_ready"], 1)
                dve.wait_ge(s["y_ready"], e + 1)
                normalise(e, "n_", y[:], z[:]).then_inc(s["n_norm"], 1)
                dve.wait_ge(s["n_norm"], el + 1)
                v.tensor_tensor(z2[:], z[:], of(gamma_b), ALU.mult).then_inc(s["n_gamma"], 1)
                dve.wait_ge(s["n_gamma"], el + 1)
                v.tensor_tensor(z3[:], z2[:], of(beta_b), ALU.add).then_inc(s["n_beta"], 1)
                dve.wait_ge(s["n_beta"], el + 1)
                v.tensor_scalar(zm[:], z3[:], 0.0, None, ALU.min).then_inc(s["n_min"], 1)
                dve.wait_ge(s["n_exp"], el + 1)
                v.scalar_tensor_tensor(out=z[:], in0=z3[:], scalar=0.0, in1=ze[:], op0=ALU.max, op1=ALU.add).then_inc(s["n_elu"], 1)
                dve.wait_ge(s["n_elu"], el + 1)
                if out_sem is not None:
                    dve.wait_ge(s["xn_tr"], e)
                    dve.wait_ge(s["xn_stored"], e)
                m = v.scalar_tensor_tensor(out=out_ap, in0=z[:], scalar=-1.0, in1=xt, op0=ALU.add, op1=ALU.add)
                return m.then_inc(s["xn_ready"], 1)

            with dve.Fori(0, L - 1) as l:
                lm = entry(dve, l + T_LM, 0, MAXS)
                dve.wait_ge(s["h_out"], (l + 1) * (3 * NT))
                dve.sem_inc(s["passed"], 1)
                with dve.Fori(0, NT) as t:
                    layer_norm_elu(l, t, weigh(l, t, lm), xn[:], "xn_ready")
            lm = entry(dve, T_LM + L - 1, 0, MAXS)
            dve.wait_ge(s["h_out"], L * 3 * NT)
            dve.wait_ge(s["x1_back"], 16)
            dve.sem_inc(s["passed"], 1)

            def last(t, first=False):
                layer_norm_elu(L - 1, t, weigh(L - 1, t, lm), xo[:], None)
                dve.wait_ge(s["xn_ready"], t + (L * NT + 1))
                v.tensor_tensor(y[:], xo[:], x1[:, bass.ds(t, 1), :].rearrange("p a d -> p (a d)"), ALU.add).then_inc(s["f_sum"], 1)
                dve.wait_ge(s["f_sum"], t + 1)
                if not first:
                    dve.wait_ge(s["out_stored"], t * 16)
                normalise(t, "f_", y[:], yo[:]).then_inc(s["f_norm"], 1)
            last(0, first=True)
            with dve.Fori(1, NT) as t:
                last(t)


def kernel(x, src, dst, edge_type_4, edge_weight, L1_gnn_weights, L1_gnn_roots, L1_gnn_biases, L1_gnn_ln_gamma, L1_gnn_ln_beta):
    import numpy as np
    import concourse.bacc as bacc
    from concourse.bass_utils import run_bass_kernel_spmd

    nc = bacc.Bacc("TRN2", target_bir_lowering=False, num_devices=1)
    inputs = {"x": x, "src": src, "dst": dst, "etype": edge_type_4, "eweight": edge_weight, "weights": L1_gnn_weights,
              "roots": L1_gnn_roots, "biases": L1_gnn_biases, "gammas": L1_gnn_ln_gamma, "betas": L1_gnn_ln_beta}
    arrays, aps = {}, []
    for name, a in inputs.items():
        arrays[name] = np.ascontiguousarray(a)
        aps.append(nc.dram_tensor(name, arrays[name].shape, mybir.dt.from_np(arrays[name].dtype), kind="ExternalInput").ap())
    out = nc.dram_tensor("out", (N, D), F32, kind="ExternalOutput").ap()
    program(nc, *aps, out)
    r = run_bass_kernel_spmd(nc, [arrays], core_ids=[0])
    return r.results[0]["out"]
```

```python
import concourse.bass as bass
from concourse import mybir
from contextlib import ExitStack

F32 = mybir.dt.float32
I32 = mybir.dt.int32
BF16 = mybir.dt.bfloat16
ALU = mybir.AluOpType
ACT = mybir.ActivationFunctionType
AX = mybir.AxisListType

P = 128
N = 3125
D = 256
E = 50000
L = 4
R = 4
NT = -(-N // P)
NP = NT * P
J = 4
GE = J * P
NG = -(-E // GE)
RG = 7
assert NG % RG == 0 and NG // RG % 2 == 0
SLOTS = RG * J
CYC = NG // RG
KH = D // P
EPS = 1e-5
KEY = 4096
BIAS = 8 * J
NB = 5 * D

T_LO, T_HI, T_SB, T_GB = 0, 32, 64, 96
T_LM, T_LG, T_LC, T_P, T_W, T_REL = 128, 132, 136, 140, 144, 176
T_END = T_REL + NG


def program(nc, x, src, dst, etype, eweight, weights, roots, biases, gammas, betas, out):
    h_rows = [nc.dram_tensor(f"h_rows{i}", [NP, R * D], F32, kind="Internal").ap() for i in range(2)]

    x1_rows = nc.dram_tensor("x1_rows", [P, NT * D], F32, kind="Internal").ap()

    ctx = ExitStack()
    with ctx:
        def sb(name, shape, dt=F32):
            return ctx.enter_context(nc.sbuf_tensor(name, shape, dt))

        def pb(name):
            return ctx.enter_context(nc.psum_tensor(name, [P, 512], F32))

        def sem(name):
            return ctx.enter_context(nc.semaphore(name))

        X = sb("X", [P, NT, D])
        base = sb("base", [P, NT, D])
        wts = sb("wts", [P, L, KH, NB])
        x1 = wts[:].rearrange("p l k n -> p (l k n)")[:, 0:NT * D].rearrange("p (t d) -> p t d", d=D)
        ring = sb("ring", [P, SLOTS, D])
        ringf = ring[:].rearrange("p s d -> p (s d)")
        bias_b = sb("bias_b", [P, L, D])
        gamma_b = sb("gamma_b", [P, L, D])
        beta_b = sb("beta_b", [P, L, D])
        nat_dst_i = ringf[0:NG, 0:512].bitcast(I32)
        nat_src_i = ringf[0:NG, 512:1024].bitcast(I32)
        nat_typ_i = ringf[0:NG, 1024:1536].bitcast(I32)
        nat_w = ringf[0:NG, 1536:2048]
        nat_src = ringf[0:NG, 2048:2560]
        nat_typ = ringf[0:NG, 2560:3072]
        nat_idx = ringf[0:NG, 3072:3584]
        nat_key = ringf[0:NG, 3584:4096]
        key_row = ringf[0:NG, 4096:4608]
        later = ringf[:, 4608:5120]
        OS = ringf[:, 5120:6144].rearrange("p (j n) -> p j n", j=J)
        OD = ringf[:, 6144:7168].rearrange("p (j c n) -> p j c n", j=J, c=2)
        nat_dst = sb("nat_dst", [NG, GE])
        ecol = sb("ecol", [P, NG + 1, 4, J])
        idx = sb("idx", [P, (NG + RG) * J], I32)
        ixb = sb("ixb", [P, 2, SLOTS], I32)
        toh = sb("toh", [P, NG, J, R], BF16)
        gcol = sb("gcol", [P, 4, J])
        S = sb("S", [P, J, P])
        dist = sb("dist", [P, J, P])
        C = sb("C", [P, J, P], BF16)
        ST = sb("ST", [P, J, P], BF16)
        Wm = sb("Wm", [P, KH, D])
        dupw = sb("dupw", [P, GE * (J + 1) // 2], BF16)
        dup = sb("dup", [P, J])
        wlast = sb("wlast", [P, J])
        junk = sb("junk", [P, GE])
        ident = sb("ident", [P, P])
        ident_h = sb("ident_h", [P, P], BF16)
        ones = sb("ones", [P, P])
        iota = sb("iota", [P, D])
        iota_t = sb("iota_t", [P, P])
        pidx = sb("pidx", [P, 1])
        pnode = sb("pnode", [P, NT])
        tbase = sb("tbase", [P, NT])
        tri = sb("tri", [P, NT])
        grow = sb("grow", [P, NG])
        nxt_i = sb("nxt_i", [NG, 1], I32)
        nxt = sb("nxt", [NG, 1])
        cmp = sb("cmp", [NG, 64])
        bad = sb("bad", [NG, 3])
        colv = sb("colv", [NT, 16])
        rowv = sb("rowv", [1, 8])
        roww = sb("roww", [1, NT])
        relr = sb("relr", [1, NG])
        relr2 = sb("relr2", [1, NG])
        lscr = sb("lscr", [1, L])
        zeros = sb("zeros", [P, D], BF16)
        xcur = sb("xcur", [P, D])
        xo = sb("xo", [P, D])
        ybase = sb("ybase", [P, D])
        z2 = sb("z2", [P, D])
        z3 = sb("z3", [P, D])
        relw = sb("relw", [NT, NG])
        relx = sb("relx", [NT, NG])
        tabf = sb("tabf", [1, T_END])
        tab = sb("tab", [1, T_END], I32)
        invd = sb("invd", [P, R])
        cntm = sb("cntm", [P, R])
        inv3 = sb("inv3", [P, 3, R], BF16)
        inv_r1 = sb("inv_r1", [P, R])
        inv_r2 = sb("inv_r2", [P, R])
        prod = sb("prod", [P, J, 3 * R])
        psum4 = sb("psum4", [P, J])
        y = sb("y", [P, D])
        z = sb("z", [P, D])
        zm = sb("zm", [P, D])
        ze = sb("ze", [P, D])
        xn = sb("xn", [P, D])
        xnT = sb("xnT", [P, KH, P])
        xT = sb("xT", [P, KH, P])
        hst = sb("hst", [P, R * D])
        yo = sb("yo", [P, D])
        st6 = sb("st6", [P, 6])
        mv = sb("mv", [P, 2])
        veps = sb("veps", [P, 1])
        half_bits = sb("half_bits", [P, 1], I32)
        rs = [sb(f"rs{k}", [P, 1]) for k in range(4)]
        rsv = [sb(f"rsv{k}", [P, 1]) for k in range(3)]
        rsh = [sb(f"rsh{k}", [P, 1]) for k in range(3)]

        acc = pb("acc")
        tr = pb("tr")
        hp = [pb(f"hp{i}") for i in range(3)]
        rowb = pb("rowb")
        pw = ctx.enter_context(nc.psum_tensor("pw", [P, KH, 512], F32))
        cnt_ps = pw[:, 0, 0:R]
        inv_ps = pw[:, 1, 0:J * 3 * R].rearrange("p (j c) -> p j c", j=J)
        ST_ps = rowb[:].bitcast(BF16)[:, 0:J * P]

        names = """ld_nat_a ld_nat_b ld_nxt ld_x ld_w ld_par nat_zero ground made nat_conv nat_join col_tr col_out
                   tb_cmp tb_cols tb_rows tb_table tab_ready
                   wm_zero key_masked key_row_ready w_ready w_cols w_dup w_last w_hot w_mm w_upd
                   xcur_ready x_tr xT_ready x_mm
                   cnt_iota cnt_S cnt_mm cnt_max inv_full inv_ready inv_zero inv_S inv_tr ST_ready
                   inv_all inv_mm inv_prod inv_sum inv_upd
                   iota_ready S_dist S_ready agg_mm idx_copied tiles_landed passed
                   y_based y_ready n_stats n_mv n_newton n_gamma n_beta n_min n_exp n_elu
                   xn_ready xn_stored xn_tr xnT_ready h_mm h_out h_stored
                   x1_saved x1_back f_sum f_stats f_mv f_newton f_norm out_stored""".split()
        s = {n: sem(n) for n in names}
        landed = [sem(f"landed{k}") for k in range(SLOTS)]

        block = ctx.enter_context(nc.Block())

        MAXS = NT * NG * L

        def entry(eng, col, lo, hi):
            return eng.value_load(tab[0:1, bass.ds(col, 1)], min_val=lo, max_val=hi)

        def tile_bounds(eng, t):
            return entry(eng, t + T_LO, 0, NG - 2), entry(eng, t + T_HI, 2, NG), entry(eng, t + T_SB, 0, MAXS)

        @block.sync
        def _(sp):
            sp.wait_ge(s["nat_zero"], 5)
            full, rest = (NG - 1) * GE, E - (NG - 1) * GE
            for a, b in ((dst, nat_dst_i), (src, nat_src_i), (etype, nat_typ_i), (eweight, nat_w)):
                sp.dma_start(b[0:NG - 1, :], a[0:full].rearrange("(g e) -> g e", e=GE)).then_inc(s["ld_nat_a"], 16)
                sp.dma_start(b[NG - 1:NG, 0:rest], a[full:E].rearrange("(g e) -> g e", e=rest)).then_inc(s["ld_nat_b"], 16)
            sp.dma_start(nxt_i[0:NG - 2, :], dst[GE:full].rearrange("(g e) -> g e", e=GE)[:, 0:1],
                         allow_slow_non_contiguous=True).then_inc(s["ld_nxt"], 16)
            sp.dma_start(nxt_i[NG - 2:NG - 1, :], dst[full:full + 1].rearrange("(g e) -> g e", e=1)).then_inc(s["ld_nxt"], 16)
            sp.dma_start(X[:, 0:NT - 1, :], x[0:(NT - 1) * P, :].rearrange("(t p) d -> p t d", p=P)).then_inc(s["ld_x"], 16)
            sp.dma_start(X[0:N - (NT - 1) * P, NT - 1, :], x[(NT - 1) * P:N, :]).then_inc(s["ld_x"], 16)
            for l in range(L):
                for k in range(KH):
                    for r in range(R):
                        sp.dma_start(wts[:, l, k, r * D:(r + 1) * D], weights[l, r, k * P:(k + 1) * P, :]).then_inc(s["ld_w"], 16)
                    sp.dma_start(wts[:, l, k, R * D:NB], roots[l, k * P:(k + 1) * P, :]).then_inc(s["ld_w"], 16)
            for a, b in ((biases, bias_b), (gammas, gamma_b), (betas, beta_b)):
                sp.dma_start(b[:], a.rearrange("(o l) d -> o l d", o=1).to_broadcast([P, L, D])).then_inc(s["ld_par"], 16)

            sp.wait_ge(s["tab_ready"], 1)
            passes = entry(sp, T_P, 1, NT)
            with sp.Fori(0, L) as l:
                lc = entry(sp, l + T_LC, 0, L * NT * CYC)
                with sp.Fori(0, passes) as p:
                    with sp.Fori(0, CYC) as c:
                        for k in range(SLOTS):
                            sp.wait_ge(landed[k], (lc + p * CYC + c + 1) * 16)
                            sp.sem_inc(s["tiles_landed"], 1)

        @block.gpsimd
        def _(pool):
            pool.memset(nat_dst_i, NP).then_inc(s["nat_zero"], 1)
            pool.memset(nat_src_i, 0).then_inc(s["nat_zero"], 1)
            pool.memset(nat_typ_i, 0).then_inc(s["nat_zero"], 1)
            pool.memset(nat_w, 0.0).then_inc(s["nat_zero"], 1)
            pool.memset(X[:, NT - 1, :], 0.0)
            pool.memset(nxt_i[:], NP).then_inc(s["nat_zero"], 1)
            pool.memset(ident[:], 0.0)
            pool.memset(ones[:], 1.0)
            pool.memset(later, 1.0)
            pool.memset(tri[:], 0.0)
            pool.memset(zeros[:], 0.0)
            pool.iota(iota[:], [[1, D]], base=0, channel_multiplier=0, allow_small_or_imprecise_dtypes=True)
            pool.iota(pnode[:], [[P, NT]], base=0, channel_multiplier=1, allow_small_or_imprecise_dtypes=True)
            pool.iota(tbase[:], [[P, NT]], base=0, channel_multiplier=0, allow_small_or_imprecise_dtypes=True)
            pool.iota(grow[:], [[1, NG]], base=1 - RG, channel_multiplier=0, allow_small_or_imprecise_dtypes=True).then_inc(s["ground"], 1)
            pool.wait_ge(s["ground"], 1)
            pool.affine_select(out=ident[:], in_=ident[:], compare_op=ALU.not_equal, fill=1.0, base=0,
                               pattern=[[-1, P]], channel_multiplier=1)
            pool.affine_select(out=later, in_=later, compare_op=ALU.is_gt, fill=0.0, base=0,
                               pattern=[[1, GE]], channel_multiplier=-1)
            pool.affine_select(out=tri[:], in_=tri[:], compare_op=ALU.is_ge, fill=1.0, base=0,
                               pattern=[[-1, NT]], channel_multiplier=1).then_inc(s["made"], 1)

            pool.wait_ge(s["w_mm"], 1)
            pool.wait_ge(s["w_ready"], 1)
            passes = entry(pool, T_P, 1, NT)
            def gathers(l, h_gather):
                pool.wait_ge(s["h_stored"], (l + 1) * (16 * NT))
                pool.sem_inc(s["passed"], 1)
                lm = entry(pool, l + T_LM, 0, MAXS)
                lc = entry(pool, l + T_LC, 0, L * NT * CYC)
                with pool.Fori(0, passes) as p:
                    with pool.Fori(0, CYC // 2) as c2:
                        for b in range(2):
                            c = c2 * 2 + b
                            q = lc + p * CYC + c
                            pool.wait_ge(s["idx_copied"], q + 1)
                            for g in range(RG):
                                rel = entry(pool, c * RG + (T_REL + g), 1, MAXS * J)
                                pool.wait_ge(s["agg_mm"], (lm + p * NG) * J + rel)
                                pool.sem_inc(s["passed"], 1)
                                if g == RG - 1:
                                    pool.tensor_copy(ixb[:, 1 - b, :], idx[:, bass.ds(c * SLOTS + SLOTS, SLOTS)]).then_inc(s["idx_copied"], 1)
                                for j in range(J):
                                    k = g * J + j
                                    pool.indirect_dma_start(ring[:, k, :], None, h_gather,
                                                            bass.IndirectOffsetOnAxis(ap=ixb[:, b, k:k + 1], axis=0)).then_inc(landed[k], 16)

            pool.tensor_copy(ixb[:, 0, :], idx[:, 0:SLOTS]).then_inc(s["idx_copied"], 1)
            with pool.Fori(0, L // 2) as two:
                for half in range(2):
                    gathers(two * 2 + half, h_rows[half].rearrange("n (r d) -> (n r) d", r=R))

        @block.tensor
        def _(pe):
            pe.sem_inc(s["agg_mm"], BIAS)
            pe.sem_inc(s["cnt_mm"], J)
            pe.sem_inc(s["cnt_S"], J)
            pe.sem_inc(s["inv_tr"], J)
            pe.sem_inc(s["inv_S"], J)
            pe.sem_inc(s["inv_mm"], 1)
            pe.sem_inc(s["inv_prod"], 1)
            pe.sem_inc(s["inv_upd"], 1)
            pe.sem_inc(s["ST_ready"], 1)
            pe.sem_inc(s["S_ready"], J)
            pe.sem_inc(s["tiles_landed"], J)
            pe.wait_ge(s["made"], 1)

            pe.wait_ge(s["nat_join"], 2)
            for a, arr in enumerate((nat_dst[:], nat_src, nat_key, nat_w, nat_idx, nat_typ)):
                bank = (tr, rowb)[a % 2]
                if a >= 2:
                    pe.wait_ge(s["col_out"], a - 1)
                for j in range(J):
                    m = nc.tensor.transpose(bank[:, j * P:j * P + NG], arr[:, j * P:(j + 1) * P], ident[0:NG, 0:NG])
                m.then_inc(s["col_tr"], 1)

            pe.wait_ge(s["tb_cmp"], 6)
            nc.tensor.matmul(acc[0:NT, 0:1], cmp[:, 0:NT], ones[0:NG, 0:1], start=True, stop=True)
            nc.tensor.matmul(acc[0:NT, 8:9], cmp[:, 32:32 + NT], ones[0:NG, 0:1], start=True, stop=True)
            nc.tensor.matmul(acc[0:NT, 16:17], ones[0:NG, 0:NT], bad[:, 2:3], start=True, stop=True).then_inc(s["tb_rows"], 1)
            pe.wait_ge(s["tb_cols"], 16)
            nc.tensor.matmul(acc[0:1, 32:32 + NT], colv[:, 6:7], ident[0:NT, 0:NT], start=True, stop=True)
            nc.tensor.matmul(acc[0:1, 64:64 + NT], colv[:, 8:9], ident[0:NT, 0:NT], start=True, stop=True)
            nc.tensor.matmul(acc[0:1, 96:96 + NT], colv[:, 9:10], tri[0:NT, :], start=True, stop=False)
            nc.tensor.matmul(acc[0:1, 96:96 + NT], colv[:, 10:11], ident[0:NT, 0:NT], start=False, stop=True)
            nc.tensor.matmul(acc[0:1, 128:129], colv[:, 9:10], ones[0:NT, 0:1], start=True, stop=True)
            nc.tensor.matmul(acc[0:1, 132:133], colv[0:1, 3:4], ones[0:1, 0:1], start=True, stop=True)
            nc.tensor.matmul(acc[0:1, 160:160 + NG], ones[0:NT, 0:1], relx[:], start=True, stop=True).then_inc(s["tb_rows"], 1)

            pe.wait_ge(s["tab_ready"], 1)
            for t in range(KH):
                lo_t, end_t, sb_t = tile_bounds(pe, t)
                with pe.Fori(lo_t, end_t) as g:
                    w = sb_t + g
                    pe.wait_ge(s["key_masked"], w + 1)
                    nc.tensor.matmul(rowb[:], ones[0:NG, :], key_row, start=True, stop=True).then_inc(s["key_row_ready"], 1)
                    for j in range(J):
                        pe.wait_ge(s["w_hot"], w * J + (j + 1))
                        for k in range(KH):
                            m = nc.tensor.matmul(pw[:, k, 0:2 * P], OS[:, j, k * P:(k + 1) * P],
                                                 OD[:, j, :, :].rearrange("p c n -> p (c n)"), start=j == 0, stop=j == J - 1)
                    m.then_inc(s["w_mm"], 1)

            def turn(e):
                pe.wait_ge(s["xn_ready"], e + 1)
                for k in range(KH):
                    m = nc.tensor.transpose(tr[:, k * P:(k + 1) * P], xn[:, k * P:(k + 1) * P], ident[:])
                m.then_inc(s["xn_tr"], 1)

            def node_products(e, layer, first=False):
                if not first:
                    pe.wait_ge(s["h_out"], e * 3)
                pe.wait_ge(s["xnT_ready"], e + 1)
                for b, (c0, c1) in enumerate(((0, 512), (512, 1024), (1024, NB))):
                    for k in range(KH):
                        rhs = wts[:, bass.ds(layer, 1), k, c0:c1].rearrange("p a c -> p (a c)")
                        m = nc.tensor.matmul(hp[b][:, 0:c1 - c0], xnT[:, k, :], rhs, start=k == 0, stop=k == KH - 1)
                    m.then_inc(s["h_mm"], 1)

            def first_product(t, first=False):
                pe.wait_ge(s["xcur_ready"], t + 1)
                for k in range(KH):
                    m = nc.tensor.transpose(tr[:, D + k * P:D + (k + 1) * P], xcur[:, k * P:(k + 1) * P], ident[:])
                m.then_inc(s["x_tr"], 1)
                if not first:
                    pe.wait_ge(s["y_ready"], t)
                pe.wait_ge(s["xT_ready"], t + 1)
                for k in range(KH):
                    m = nc.tensor.matmul(acc[:, 0:D], xT[:, k, :], Wm[:, k, :], start=k == 0, stop=k == KH - 1)
                m.then_inc(s["x_mm"], 1)

            pe.wait_ge(s["w_ready"], 1)
            pe.wait_ge(s["ld_w"], 16 * L * KH * (R + 1))
            first_product(0, first=True)
            first_product(1)
            turn(0)
            node_products(0, 0, first=True)
            with pe.Fori(2, NT) as t:
                first_product(t)
                turn(t - 1)
                node_products(t - 1, 0)
            turn(NT - 1)
            node_products(NT - 1, 0)

            pe.wait_ge(s["inv_zero"], 2)
            with pe.Fori(0, NT) as t:
                lo_t, end_t, sb_t = tile_bounds(pe, t)
                nc.tensor.matmul(cnt_ps, zeros[:, 0:P], zeros[:, 0:R], start=True, stop=True)
                with pe.Fori(lo_t, end_t) as g:
                    for j in range(J):
                        pe.wait_ge(s["cnt_S"], (sb_t + g) * J + (J + j + 1))
                        nc.tensor.matmul(cnt_ps, C[:, j, :], toh[:, bass.ds(g, 1), j, :].rearrange("p a r -> p (a r)"),
                                         start=False, stop=True, skip_group_check=True).then_inc(s["cnt_mm"], 1)
                def turned(q):
                    pe.wait_ge(s["ST_ready"], q + 1)
                    for j in range(J):
                        pe.wait_ge(s["inv_S"], q * J + (J + j + 1))
                        nc.tensor.transpose(ST_ps[:, j * P:(j + 1) * P], C[:, j, :], ident_h[:]).then_inc(s["inv_tr"], 1)

                turned(sb_t + lo_t + t)
                pe.wait_ge(s["inv_ready"], t + 1)
                pe.sem_inc(s["passed"], 1)
                with pe.Fori(lo_t, end_t) as g:
                    w = sb_t + g
                    turned(w + t + 1)
                    pe.wait_ge(s["inv_prod"], w + 1)
                    for j in range(J):
                        m = nc.tensor.matmul(inv_ps[:, j, :], ST[:, j, :], inv3[:].rearrange("p c r -> p (c r)"), start=True, stop=True)
                    m.then_inc(s["inv_mm"], 1)

            def aggregate(l, t, lm, lg, before_last=None):
                lo_t, end_t, sb_t = tile_bounds(pe, t)
                gb_t = entry(pe, t + T_GB, 0, MAXS * J)
                pe.wait_ge(s["y_ready"], l * NT + (t + NT))
                nc.tensor.matmul(acc[:, 0:D], zeros[:, 0:P], zeros[:], start=True, stop=True)

                def group(g, after):
                    for j in range(J):
                        pe.wait_ge(s["S_ready"], (lm + sb_t + after) * J + (j + 1))
                        pe.wait_ge(s["tiles_landed"], lg + gb_t + after * J + (j + 1))
                        nc.tensor.matmul(acc[:, 0:D], S[:, j, :],
                                         ring[:, bass.ds(g % RG * J + j, 1), :].rearrange("p a d -> p (a d)"),
                                         start=False, stop=True, skip_group_check=True).then_inc(s["agg_mm"], 1)

                with pe.Fori(lo_t, end_t - 1) as g:
                    group(g, g + 1)
                if before_last is not None:
                    before_last()
                group(end_t - 1, end_t)

            with pe.Fori(0, L - 1) as l:
                lm = entry(pe, l + T_LM, 0, MAXS)
                lg = entry(pe, l + T_LG, 0, MAXS * J)
                aggregate(l, 0, lm, lg)
                with pe.Fori(1, NT) as t:
                    aggregate(l, t, lm, lg, lambda: turn(l * NT + (t + NT - 1)))
                    node_products(l * NT + (t + NT - 1), l + 1)
                turn(l * NT + (2 * NT - 1))
                node_products(l * NT + (2 * NT - 1), l + 1)
            lm = entry(pe, T_LM + L - 1, 0, MAXS)
            lg = entry(pe, T_LG + L - 1, 0, MAXS * J)
            with pe.Fori(0, NT) as t:
                aggregate(L - 1, t, lm, lg)

        @block.scalar
        def _(act):
            def transposed(e, first=False):
                act.wait_ge(s["xn_tr"], e + 1)
                if not first:
                    act.wait_ge(s["h_mm"], e * 3)
                nc.scalar.activation(xnT[:].rearrange("p k n -> p (k n)"), tr[:, 0:D], ACT.Copy).then_inc(s["xnT_ready"], 1)

            def products_out(e, t, half, first=False):
                act.wait_ge(s["h_mm"], e * 3 + 1)
                if not first:
                    act.wait_ge(s["h_stored"], e * 16)
                nc.scalar.activation(hst[:, 0:512], hp[0][:], ACT.Copy).then_inc(s["h_out"], 1)
                act.wait_ge(s["h_mm"], e * 3 + 2)
                nc.scalar.activation(hst[:, 512:1024], hp[1][:], ACT.Copy).then_inc(s["h_out"], 1)
                act.wait_ge(s["h_mm"], e * 3 + 3)
                act.sem_inc(s["passed"], 1)
                nc.scalar.activation(base[:, bass.ds(t, 1), :].rearrange("p a d -> p (a d)"), hp[2][:, 0:D],
                                     ACT.Copy).then_inc(s["h_out"], 1)
                act.wait_ge(s["h_out"], e * 3 + 2)
                act.dma_start(h_rows[half][bass.ds(t * P, P), :], hst[:]).then_inc(s["h_stored"], 16)

            def store_xn(e, t):
                act.wait_ge(s["xn_ready"], e + 1)
                act.sem_inc(s["passed"], 1)
                nc.scalar.activation(X[:, bass.ds(t, 1), :].rearrange("p a d -> p (a d)"), xn[:], ACT.Copy).then_inc(s["xn_stored"], 1)

            def current_x(t, first=False):
                if not first:
                    act.wait_ge(s["x_tr"], t)
                    act.sem_inc(s["passed"], 1)
                nc.scalar.activation(xcur[:], X[:, bass.ds(t, 1), :].rearrange("p a d -> p (a d)"), ACT.Copy).then_inc(s["xcur_ready"], 1)

            def x_transposed(t, first=False):
                act.wait_ge(s["x_tr"], t + 1)
                if not first:
                    act.wait_ge(s["x_mm"], t)
                nc.scalar.activation(xT[:].rearrange("p k n -> p (k n)"), tr[:, D:2 * D], ACT.Copy).then_inc(s["xT_ready"], 1)

            act.wait_ge(s["ld_x"], 32)
            act.wait_ge(s["w_ready"], 1)
            current_x(0, first=True)
            x_transposed(0, first=True)
            current_x(1)
            store_xn(0, 0)
            x_transposed(1)
            transposed(0, first=True)
            current_x(2)
            store_xn(1, 1)
            products_out(0, 0, 0, first=True)
            with act.Fori(2, NT - 1) as t:
                x_transposed(t)
                transposed(t - 1)
                current_x(t + 1)
                store_xn(t, t)
                products_out(t - 1, t - 1, 0)
            t = NT - 1
            x_transposed(t)
            transposed(t - 1)
            store_xn(t, t)
            products_out(t - 1, t - 1, 0)
            transposed(t)
            products_out(t, t, 0)

            act.wait_ge(s["xn_stored"], NT)
            act.dma_start(x1_rows, X[:].rearrange("p t d -> p (t d)")).then_inc(s["x1_saved"], 16)
            act.wait_ge(s["x1_saved"], 16)
            act.sem_inc(s["passed"], 1)

            def ST_out(w, t):
                act.wait_ge(s["inv_tr"], (w + t) * J + 2 * J)
                act.wait_ge(s["inv_mm"], w + 1)
                nc.scalar.activation(ST[:].rearrange("p j n -> p (j n)"), ST_ps, ACT.Copy).then_inc(s["ST_ready"], 1)

            with act.Fori(0, NT) as t:
                lo_t, end_t, sb_t = tile_bounds(act, t)
                ST_out(sb_t + lo_t, t)
                with act.Fori(lo_t, end_t) as g:
                    ST_out(sb_t + g + 1, t)

            def elu_exp(el):
                act.wait_ge(s["n_min"], el + 1)
                nc.scalar.activation(ze[:], zm[:], ACT.Exp).then_inc(s["n_exp"], 1)

            def node_numbers(l, t, bounds, lm):
                act.wait_ge(s["S_ready"], (lm + bounds[2] + bounds[0]) * J + J)
                act.sem_inc(s["passed"], 1)
                nc.scalar.activation(iota_t[:], iota[:, 0:P], ACT.Identity, bias=tbase[:, bass.ds(t, 1)]).then_inc(s["iota_ready"], 1)
                act.wait_ge(s["iota_ready"], l * NT + (t + 1))
                act.sem_inc(s["passed"], 1)

            def weigh(g, w):
                def column(a, j):
                    return ecol[:, bass.ds(g, 1), a, j:j + 1].rearrange("p a j -> p (a j)")
                act.wait_ge(s["S_ready"], w * J + J)
                act.sem_inc(s["passed"], 1)
                for j in range(J):
                    nc.scalar.activation(dist[:, j, :], iota_t[:], ACT.Abs, bias=column(0, j), scale=-1.0).then_inc(s["S_dist"], 1)
                for j in range(J):
                    act.wait_ge(s["S_dist"], w * J + (j + 1))
                    act.wait_ge(s["agg_mm"], w * J + (j + 1 + BIAS - J))
                    act.sem_inc(s["passed"], 1)
                    nc.scalar.activation(S[:, j, :], dist[:, j, :], ACT.Relu, bias=column(1, j), scale=column(2, j)).then_inc(s["S_ready"], 1)

            def weigh_first(l, t, bounds, lm):
                node_numbers(l, t, bounds, lm)
                weigh(bounds[0], lm + bounds[2] + bounds[0])

            def weigh_rest(bounds, lm):
                lo_t, end_t, sb_t = bounds
                with act.Fori(lo_t + 1, end_t) as g:
                    weigh(g, lm + sb_t + g)

            act.wait_ge(s["inv_all"], 1)
            act.sem_inc(s["passed"], 1)
            for l in range(L - 1):
                half = (l + 1) % 2
                lm = entry(act, T_LM + l, 0, MAXS)
                bounds = tile_bounds(act, 0)
                weigh_first(l, 0, bounds, lm)
                weigh_rest(bounds, lm)

                def step(t, first=False):
                    bounds = tile_bounds(act, t)
                    weigh_first(l, t, bounds, lm)
                    if not first:
                        products_out(l * NT + (t + NT - 2), t - 2, half)
                    elu_exp(l * NT + (t - 1))
                    weigh_rest(bounds, lm)
                    transposed(l * NT + (t + NT - 1))
                    store_xn(l * NT + (t + NT - 1), t - 1)

                step(1, first=True)
                with act.Fori(2, NT) as t:
                    step(t)
                products_out(l * NT + (2 * NT - 2), NT - 2, half)
                elu_exp(l * NT + (NT - 1))
                transposed(l * NT + (2 * NT - 1))
                store_xn(l * NT + (2 * NT - 1), NT - 1)
                products_out(l * NT + (2 * NT - 1), NT - 1, half)

            act.wait_ge(s["h_mm"], L * NT * 3)
            act.dma_start(x1.rearrange("p t d -> p (t d)"), x1_rows).then_inc(s["x1_back"], 16)

            def store_out(t):
                act.wait_ge(s["f_norm"], t + 1)
                act.dma_start(out[bass.ds(t * P, P), :], yo[:]).then_inc(s["out_stored"], 16)

            def last_step(t, first=False):
                bounds = tile_bounds(act, t)
                weigh_first(L - 1, t, bounds, lm)
                if not first:
                    store_out(t - 2)
                elu_exp((L - 1) * NT + (t - 1))
                weigh_rest(bounds, lm)

            lm = entry(act, T_LM + L - 1, 0, MAXS)
            bounds = tile_bounds(act, 0)
            weigh_first(L - 1, 0, bounds, lm)
            weigh_rest(bounds, lm)
            last_step(1, first=True)
            with act.Fori(2, NT) as t:
                last_step(t)
            store_out(NT - 2)
            elu_exp(L * NT - 1)
            act.wait_ge(s["f_norm"], NT)
            act.dma_start(out[(NT - 1) * P:N, :], yo[0:N - (NT - 1) * P, :]).then_inc(s["out_stored"], 16)
            act.wait_ge(s["out_stored"], 16 * NT)

        @block.vector
        def _(dve):
            v = nc.vector
            dve.wait_ge(s["ld_nat_a"], 16 * 4)
            dve.wait_ge(s["ld_nat_b"], 16 * 4)
            v.tensor_copy(nat_dst[:], nat_dst_i)
            v.tensor_copy(nat_src, nat_src_i)
            v.tensor_copy(nat_typ, nat_typ_i).then_inc(s["nat_conv"], 1)
            dve.wait_ge(s["nat_conv"], 1)
            v.scalar_tensor_tensor(out=nat_key, in0=nat_src, scalar=float(KEY), in1=nat_dst[:], op0=ALU.mult, op1=ALU.add).then_inc(s["nat_join"], 1)
            v.scalar_tensor_tensor(out=nat_idx, in0=nat_src, scalar=float(R), in1=nat_typ, op0=ALU.mult, op1=ALU.add).then_inc(s["nat_join"], 1)

            dve.wait_ge(s["made"], 1)
            dve.wait_ge(s["ld_nxt"], 32)
            v.tensor_scalar(cmp[:, 0:NT], tbase[0:NG, :], nat_dst[:, 0:1], float(-P), ALU.subtract, ALU.is_gt).then_inc(s["tb_cmp"], 1)
            v.tensor_scalar(cmp[:, 32:32 + NT], tbase[0:NG, :], nat_dst[:, GE - 1:GE], 0.0, ALU.subtract, ALU.is_gt).then_inc(s["tb_cmp"], 1)
            v.tensor_tensor(junk[0:NG, 0:GE - 1], nat_dst[:, 1:GE], nat_dst[:, 0:GE - 1], ALU.is_lt)
            v.tensor_copy(nxt[:], nxt_i[:]).then_inc(s["tb_cmp"], 1)
            dve.wait_ge(s["tb_cmp"], 3)
            v.tensor_reduce(bad[:, 0:1], junk[0:NG, 0:GE - 1], AX.X, ALU.max).then_inc(s["tb_cmp"], 1)
            v.tensor_tensor(bad[:, 1:2], nxt[:], nat_dst[:, GE - 1:GE], ALU.is_lt).then_inc(s["tb_cmp"], 1)
            dve.wait_ge(s["tb_cmp"], 5)
            v.tensor_tensor(bad[:, 2:3], bad[:, 0:1], bad[:, 1:2], ALU.max).then_inc(s["tb_cmp"], 1)

            dup_at = [sum(GE - k * P for k in range(j)) for j in range(J + 1)]

            def columns(a, out_ap, bank):
                dve.wait_ge(s["col_tr"], a + 1)
                return v.tensor_scalar(out_ap, bank[:].rearrange("p (j g) -> p j g", j=J)[:, :, 0:NG].rearrange("p j g -> p g j"),
                                       0.0, None, ALU.add)
            for a in range(4):
                columns(a, ecol[:, 0:NG, a, :], (tr, rowb)[a % 2]).then_inc(s["col_out"], 1)
            columns(4, idx[:, 0:NG * J].rearrange("p (g j) -> p g j", j=J), tr).then_inc(s["col_out"], 1)
            dve.wait_ge(s["col_out"], 5)
            v.tensor_copy(idx[:, NG * J:(NG + RG) * J], idx[:, 0:SLOTS])
            dve.wait_ge(s["col_tr"], 6)
            for r in range(R):
                v.tensor_scalar(toh[:, :, :, r], rowb[:].rearrange("p (j g) -> p j g", j=J)[:, :, 0:NG].rearrange("p j g -> p g j"),
                                float(r), None, ALU.is_equal)

            c = lambda n: colv[:, n:n + 1]
            step = [0]

            def col(ins):
                step[0] += 1
                ins.then_inc(s["tb_cols"], 1)
                dve.wait_ge(s["tb_cols"], step[0])
            dve.wait_ge(s["tb_rows"], 1)
            col(v.tensor_scalar(c(3), acc[0:NT, 16:17], 1.0, None, ALU.min))
            col(v.tensor_scalar(c(4), c(3), -1.0, 1.0, ALU.mult, ALU.add))
            col(v.tensor_scalar(c(1), acc[0:NT, 0:1], 1.0, None, ALU.max))
            col(v.tensor_scalar(c(5), c(1), 1.0, None, ALU.subtract))
            col(v.tensor_tensor(c(0), acc[0:NT, 8:9], c(5), ALU.min))
            col(v.tensor_tensor(c(2), c(0), c(4), ALU.mult))
            col(v.tensor_scalar(c(6), c(2), float(NG - 2), None, ALU.min))
            col(v.tensor_tensor(c(7), c(1), c(4), ALU.mult))
            col(v.scalar_tensor_tensor(out=c(11), in0=c(3), scalar=float(NG), in1=c(7), op0=ALU.mult, op1=ALU.add))
            col(v.scalar_tensor_tensor(out=c(8), in0=c(6), scalar=2.0, in1=c(11), op0=ALU.add, op1=ALU.max))
            col(v.tensor_tensor(c(9), c(8), c(6), ALU.subtract))
            col(v.tensor_scalar(c(10), c(6), -1.0, None, ALU.mult))
            col(v.tensor_scalar(c(12), c(8), 1.0, None, ALU.subtract))
            col(v.tensor_scalar(c(13), c(6), 1.0, None, ALU.subtract))
            col(v.tensor_scalar(relw[:], grow[0:NT, :], c(12), c(13), ALU.min, ALU.subtract))
            col(v.tensor_scalar(relx[:], relw[:], 0.0, None, ALU.max))

            r_ = lambda n: rowv[:, n:n + 1]
            count = [0]

            def row(ins):
                count[0] += 1
                ins.then_inc(s["tb_table"], 1)
                dve.wait_ge(s["tb_table"], count[0])
            dve.wait_ge(s["tb_rows"], 2)
            row(v.memset(tabf[:], 0.0))
            row(v.tensor_scalar(r_(0), acc[0:1, 128:129], 0.0, None, ALU.add))
            row(v.tensor_scalar(r_(1), acc[0:1, 132:133], 0.0, None, ALU.add))
            row(v.tensor_scalar(r_(2), r_(1), -1.0, 1.0, ALU.mult, ALU.add))
            row(v.tensor_scalar(r_(3), r_(1), float(NT - 1), 1.0, ALU.mult, ALU.add))
            v.tensor_scalar(tabf[:, T_P:T_P + 1], r_(3), 0.0, None, ALU.add)
            v.tensor_scalar(tabf[:, T_LO:T_LO + NT], acc[0:1, 32:32 + NT], 0.0, None, ALU.add)
            v.tensor_scalar(tabf[:, T_HI:T_HI + NT], acc[0:1, 64:64 + NT], 0.0, None, ALU.add)
            v.tensor_scalar(tabf[:, T_SB:T_SB + NT], acc[0:1, 96:96 + NT], 0.0, None, ALU.add)
            row(v.tensor_scalar(roww[:], acc[0:1, 96:96 + NT], 0.0, None, ALU.add))
            v.tensor_tensor(tabf[:, T_W:T_W + NT], roww[:], acc[0:1, 32:32 + NT], ALU.add)
            v.tensor_scalar(tabf[:, T_GB:T_GB + NT], tbase[0:1, :], r_(1), float(NG * J) / P, ALU.mult, ALU.mult)
            v.tensor_scalar(tabf[:, T_LM:T_LM + L], iota[0:1, 0:L], r_(0), None, ALU.mult)
            v.tensor_scalar(tabf[:, T_LG:T_LG + L], iota[0:1, 0:L], r_(3), float(NG * J), ALU.mult, ALU.mult)
            v.tensor_scalar(tabf[:, T_LC:T_LC + L], iota[0:1, 0:L], r_(3), float(CYC), ALU.mult, ALU.mult)
            row(v.tensor_scalar(relr[:], acc[0:1, 160:160 + NG], r_(2), None, ALU.mult))
            row(v.scalar_tensor_tensor(out=relr2[:], in0=grow[0:1, :], scalar=r_(1), in1=relr[:], op0=ALU.mult, op1=ALU.add))
            row(v.tensor_scalar(tabf[:, T_REL:T_END], relr2[:], float(J), float(BIAS), ALU.mult, ALU.add))
            v.tensor_copy(ident_h[:], ident[:])
            v.memset(Wm[:], 0.0).then_inc(s["wm_zero"], 1)
            v.tensor_copy(tab[:], tabf[:]).then_inc(s["tab_ready"], 1)
            dve.wait_ge(s["tab_ready"], 1)
            dve.wait_ge(s["wm_zero"], 1)

            for t in range(KH):
                lo_t, end_t, sb_t = tile_bounds(dve, t)
                Wt = Wm[:, :, t * P:(t + 1) * P]
                with dve.Fori(lo_t, end_t) as g:
                    w = sb_t + g
                    v.tensor_scalar(key_row, nat_key, ident[0:NG, bass.ds(g, 1)], None, ALU.mult).then_inc(s["key_masked"], 1)
                    v.tensor_copy(gcol[:], ecol[:, bass.ds(g, 1), :, :].rearrange("p a c j -> p (a c) j")).then_inc(s["w_cols"], 1)
                    dve.wait_ge(s["w_cols"], w + 1)
                    dve.wait_ge(s["key_row_ready"], w + 1)
                    for j in range(J):
                        v.scalar_tensor_tensor(out=dupw[:, dup_at[j]:dup_at[j + 1]], in0=rowb[:, j * P:GE], scalar=gcol[:, 2, j:j + 1],
                                               in1=later[:, 0:GE - j * P], op0=ALU.is_equal, op1=ALU.mult,
                                               accum_out=dup[:, j:j + 1]).then_inc(s["w_dup"], 1)
                    dve.wait_ge(s["w_dup"], w * J + J)
                    v.scalar_tensor_tensor(out=wlast[:], in0=dup[:], scalar=0.0, in1=gcol[:, 3, :], op0=ALU.is_equal,
                                           op1=ALU.mult).then_inc(s["w_last"], 1)
                    dve.wait_ge(s["w_last"], w + 1)
                    for j in range(J):
                        v.tensor_scalar(OS[:, j, :], iota[:], gcol[:, 1, j:j + 1], None, ALU.is_equal)
                        v.tensor_scalar(OD[:, j, 0, :], iota[:, t * P:(t + 1) * P], gcol[:, 0, j:j + 1], None, ALU.is_equal)
                        v.tensor_scalar(OD[:, j, 1, :], iota[:, t * P:(t + 1) * P], gcol[:, 0, j:j + 1], wlast[:, j:j + 1],
                                        ALU.is_equal, ALU.mult).then_inc(s["w_hot"], 1)
                    dve.wait_ge(s["w_mm"], w + 1)
                    v.scalar_tensor_tensor(out=Wt, in0=pw[:, :, 0:P], scalar=0.0, in1=Wt, op0=ALU.is_equal,
                                           op1=ALU.mult).then_inc(s["w_upd"], 1)
                    dve.wait_ge(s["w_upd"], w * 2 + 1)
                    v.tensor_tensor(Wt, Wt, pw[:, :, P:2 * P], ALU.add).then_inc(s["w_upd"], 1)
                    dve.wait_ge(s["w_upd"], w * 2 + 2)
            v.memset(ecol[:, :, 1, :], 0.0).then_inc(s["inv_zero"], 1)
            v.memset(ecol[:, NG, 0, :], float(NP)).then_inc(s["inv_zero"], 1)
            dve.sem_inc(s["w_ready"], 1)

            def root(e, pre, between=None):
                newton = s[pre + "newton"]
                v.tensor_scalar(veps[:], mv[:, 1:2], EPS, None, ALU.add).then_inc(newton, 1)
                dve.wait_ge(newton, e * 12 + 1)
                v.tensor_scalar(half_bits[:], veps[:].bitcast(I32), 1, None, ALU.logical_shift_right).then_inc(newton, 1)
                dve.wait_ge(newton, e * 12 + 2)
                v.tensor_scalar(rs[0][:].bitcast(I32), half_bits[:], -1.0, float(0x5F3759DF), ALU.mult, ALU.add).then_inc(newton, 1)
                for k in range(3):
                    dve.wait_ge(newton, e * 12 + (3 + 3 * k))
                    v.scalar_tensor_tensor(out=rsv[k][:], in0=rs[k][:], scalar=rs[k][:], in1=veps[:], op0=ALU.mult, op1=ALU.mult).then_inc(newton, 1)
                    v.tensor_scalar(rsh[k][:], rs[k][:], -0.5, None, ALU.mult).then_inc(newton, 1)
                    if k == 0 and between is not None:
                        between()
                    dve.wait_ge(newton, e * 12 + (5 + 3 * k))
                    v.tensor_scalar(rs[k + 1][:], rsv[k][:], 3.0, rsh[k][:], ALU.subtract, ALU.mult).then_inc(newton, 1)
                dve.wait_ge(newton, e * 12 + 12)

            def statistics(e, pre, y_in):
                v.bn_stats(st6[:], y_in).then_inc(s[pre + "stats"], 1)
                dve.wait_ge(s[pre + "stats"], e + 1)
                dve.sem_inc(s["passed"], 1)
                v.bn_aggr(mv[:], st6[:]).then_inc(s[pre + "mv"], 1)
                dve.wait_ge(s[pre + "mv"], e + 1)

            def normalise(e, pre, y_in, out_ap):
                statistics(e, pre, y_in)
                root(e, pre)
                return v.tensor_scalar(out_ap, y_in, mv[:, 0:1], rs[3][:], ALU.subtract, ALU.mult)

            def first_norm(t, first=False):
                dve.wait_ge(s["x_mm"], t + 1)
                v.tensor_tensor(y[:], acc[:, 0:D], X[:, bass.ds(t, 1), :].rearrange("p a d -> p (a d)"), ALU.add).then_inc(s["y_ready"], 1)
                dve.wait_ge(s["y_ready"], t + 1)
                if not first:
                    dve.wait_ge(s["xn_tr"], t)
                    dve.wait_ge(s["xn_stored"], t)
                normalise(t, "n_", y[:], xn[:]).then_inc(s["xn_ready"], 1)
            first_norm(0, first=True)
            with dve.Fori(1, NT) as t:
                first_norm(t)

            dve.wait_ge(s["inv_zero"], 2)
            dve.wait_ge(s["y_ready"], NT)
            with dve.Fori(0, NT) as t:
                lo_t, end_t, sb_t = tile_bounds(dve, t)
                q0 = sb_t + lo_t + t
                dve.wait_ge(s["cnt_S"], (sb_t + lo_t) * J + J)
                dve.wait_ge(s["inv_S"], q0 * J + J)
                v.tensor_scalar(iota_t[:], iota[:, 0:P], tbase[:, bass.ds(t, 1)], None, ALU.add).then_inc(s["cnt_iota"], 1)
                dve.wait_ge(s["cnt_iota"], t + 1)
                dve.sem_inc(s["passed"], 1)

                def one_hot(g, j):
                    return v.tensor_scalar(C[:, j, :], iota_t[:], ecol[:, bass.ds(g, 1), 0, j:j + 1].rearrange("p a j -> p (a j)"),
                                           None, ALU.is_equal)

                dve.wait_ge(s["inv_tr"], q0 * J + J)
                dve.sem_inc(s["passed"], 1)
                with dve.Fori(lo_t, end_t) as g:
                    w = sb_t + g
                    for j in range(J):
                        dve.wait_ge(s["cnt_mm"], w * J + (j + 1))
                        one_hot(g, j).then_inc(s["cnt_S"], 1)
                dve.wait_ge(s["cnt_mm"], (sb_t + end_t) * J + J)
                for j in range(J):
                    one_hot(lo_t, j).then_inc(s["inv_S"], 1)
                v.tensor_scalar(cntm[:], cnt_ps, 1.0, None, ALU.max).then_inc(s["cnt_max"], 1)
                dve.wait_ge(s["cnt_max"], t + 1)
                dve.wait_ge(s["inv_mm"], sb_t + lo_t + 1)
                v.reciprocal(invd[:], cntm[:]).then_inc(s["inv_full"], 1)
                dve.wait_ge(s["inv_full"], t * 5 + 1)
                v.tensor_copy(inv3[:, 0, :], invd[:]).then_inc(s["inv_full"], 1)
                dve.wait_ge(s["inv_full"], t * 5 + 2)
                v.tensor_tensor(inv_r1[:], invd[:], inv3[:, 0, :], ALU.subtract).then_inc(s["inv_full"], 1)
                dve.wait_ge(s["inv_full"], t * 5 + 3)
                v.tensor_copy(inv3[:, 1, :], inv_r1[:]).then_inc(s["inv_full"], 1)
                dve.wait_ge(s["inv_full"], t * 5 + 4)
                v.tensor_tensor(inv_r2[:], inv_r1[:], inv3[:, 1, :], ALU.subtract).then_inc(s["inv_full"], 1)
                dve.wait_ge(s["inv_full"], t * 5 + 5)
                v.tensor_copy(inv3[:, 2, :], inv_r2[:]).then_inc(s["inv_ready"], 1)
                with dve.Fori(lo_t, end_t) as g:
                    w = sb_t + g
                    for j in range(J):
                        dve.wait_ge(s["inv_tr"], (w + t) * J + (J + j + 1))
                        one_hot(g + 1, j).then_inc(s["inv_S"], 1)
                    dve.wait_ge(s["inv_mm"], w + 2)
                    v.tensor_tensor(prod[:].rearrange("p j (c r) -> p j c r", r=R), inv_ps.rearrange("p j (c r) -> p j c r", r=R),
                                    toh[:, bass.ds(g, 1), :, :].rearrange("p a j r -> p (a j) r").unsqueeze(2).to_broadcast([P, J, 3, R]),
                                    ALU.mult).then_inc(s["inv_prod"], 1)
                    dve.wait_ge(s["inv_prod"], w + 2)
                    v.tensor_reduce(psum4[:], prod[:], AX.X, ALU.add).then_inc(s["inv_sum"], 1)
                    dve.wait_ge(s["inv_sum"], w + 1)
                    dve.wait_ge(s["inv_upd"], w + 1)
                    einv = ecol[:, bass.ds(g, 1), 1, :].rearrange("p a j -> p (a j)")
                    v.tensor_tensor(einv, einv, psum4[:], ALU.add).then_inc(s["inv_upd"], 1)

            dve.wait_ge(s["inv_upd"], entry(dve, T_LM + 1, 0, MAXS) + 1)
            dve.sem_inc(s["passed"], 1)
            v.tensor_scalar(ecol[:, 0:NG, 2, :], ecol[:, 0:NG, 1, :], -1.0, None, ALU.mult).then_inc(s["inv_all"], 1)

            dve.wait_ge(s["ld_par"], 48)

            def layer_norm_elu(l, t, steps, out_ap, out_sem):
                def of(a):
                    return a[:, bass.ds(l, 1), :].rearrange("p a d -> p (a d)")
                e, el = l * NT + (t + NT), l * NT + t
                xt = X[:, bass.ds(t, 1), :].rearrange("p a d -> p (a d)")
                bt = base[:, bass.ds(t, 1), :].rearrange("p a d -> p (a d)")
                v.tensor_tensor(ybase[:], bt, of(bias_b), ALU.add).then_inc(s["y_based"], 1)
                dve.wait_ge(s["y_based"], el + 1)
                dve.wait_ge(s["agg_mm"], steps * J + BIAS)
                v.tensor_tensor(y[:], acc[:, 0:D], ybase[:], ALU.add).then_inc(s["y_ready"], 1)
                dve.wait_ge(s["y_ready"], e + 1)
                statistics(e, "n_", y[:])
                root(e, "n_", lambda: v.scalar_tensor_tensor(out=z2[:], in0=y[:], scalar=mv[:, 0:1], in1=of(gamma_b),
                                                             op0=ALU.subtract, op1=ALU.mult).then_inc(s["n_gamma"], 1))
                dve.wait_ge(s["n_gamma"], el + 1)
                v.scalar_tensor_tensor(out=z3[:], in0=z2[:], scalar=rs[3][:], in1=of(beta_b), op0=ALU.mult,
                                       op1=ALU.add).then_inc(s["n_beta"], 1)
                dve.wait_ge(s["n_beta"], el + 1)
                v.tensor_scalar(zm[:], z3[:], 0.0, None, ALU.min).then_inc(s["n_min"], 1)
                v.scalar_tensor_tensor(out=z[:], in0=z3[:], scalar=0.0, in1=xt, op0=ALU.max, op1=ALU.add).then_inc(s["n_elu"], 1)
                dve.wait_ge(s["n_elu"], el + 1)
                if out_sem is not None:
                    dve.wait_ge(s["xn_tr"], e)
                    dve.wait_ge(s["xn_stored"], e)
                dve.wait_ge(s["n_exp"], el + 1)
                m = v.scalar_tensor_tensor(out=out_ap, in0=ze[:], scalar=-1.0, in1=z[:], op0=ALU.add, op1=ALU.add)
                return m.then_inc(s["xn_ready"], 1)

            with dve.Fori(0, L - 1) as l:
                lm = entry(dve, l + T_LM, 0, MAXS)
                dve.wait_ge(s["h_out"], (l + 1) * (3 * NT))
                dve.sem_inc(s["passed"], 1)
                with dve.Fori(0, NT - 1) as t:
                    layer_norm_elu(l, t, lm + entry(dve, t + (T_W + 1), 0, MAXS), xn[:], "xn_ready")
                layer_norm_elu(l, NT - 1, lm + entry(dve, T_LM + 1, 0, MAXS), xn[:], "xn_ready")
            lm = entry(dve, T_LM + L - 1, 0, MAXS)
            dve.wait_ge(s["h_out"], L * 3 * NT)
            dve.wait_ge(s["x1_back"], 16)
            dve.sem_inc(s["passed"], 1)

            def last(t, steps, first=False):
                layer_norm_elu(L - 1, t, steps, xo[:], None)
                dve.wait_ge(s["xn_ready"], t + (L * NT + 1))
                v.tensor_tensor(y[:], xo[:], x1[:, bass.ds(t, 1), :].rearrange("p a d -> p (a d)"), ALU.add).then_inc(s["f_sum"], 1)
                dve.wait_ge(s["f_sum"], t + 1)
                if not first:
                    dve.wait_ge(s["out_stored"], t * 16)
                normalise(t, "f_", y[:], yo[:]).then_inc(s["f_norm"], 1)
            last(0, lm + entry(dve, T_W + 1, 0, MAXS), first=True)
            with dve.Fori(1, NT - 1) as t:
                last(t, lm + entry(dve, t + (T_W + 1), 0, MAXS))
            last(NT - 1, lm + entry(dve, T_LM + 1, 0, MAXS))


def kernel(x, src, dst, edge_type_4, edge_weight, L1_gnn_weights, L1_gnn_roots, L1_gnn_biases, L1_gnn_ln_gamma, L1_gnn_ln_beta):
    import numpy as np
    import concourse.bacc as bacc
    from concourse.bass_utils import run_bass_kernel_spmd

    nc = bacc.Bacc("TRN2", target_bir_lowering=False, num_devices=1)
    inputs = {"x": x, "src": src, "dst": dst, "etype": edge_type_4, "eweight": edge_weight, "weights": L1_gnn_weights,
              "roots": L1_gnn_roots, "biases": L1_gnn_biases, "gammas": L1_gnn_ln_gamma, "betas": L1_gnn_ln_beta}
    arrays, aps = {}, []
    for name, a in inputs.items():
        arrays[name] = np.ascontiguousarray(a)
        aps.append(nc.dram_tensor(name, arrays[name].shape, mybir.dt.from_np(arrays[name].dtype), kind="ExternalInput").ap())
    out = nc.dram_tensor("out", (N, D), F32, kind="ExternalOutput").ap()
    program(nc, *aps, out)
    r = run_bass_kernel_spmd(nc, [arrays], core_ids=[0])
    return r.results[0]["out"]
```

```python
import concourse.bass as bass
from concourse import mybir
from contextlib import ExitStack

F32 = mybir.dt.float32
I32 = mybir.dt.int32
BF16 = mybir.dt.bfloat16
ALU = mybir.AluOpType
ACT = mybir.ActivationFunctionType
AX = mybir.AxisListType

P = 128
N = 3125
D = 256
E = 50000
L = 4
R = 4
NT = -(-N // P)
NP = NT * P
J = 4
GE = J * P
NG = -(-E // GE)
RG = 7
assert NG % RG == 0 and NG // RG % 2 == 0
SLOTS = RG * J
CYC = NG // RG
KH = D // P
EPS = 1e-5
KEY = 4096
BIAS = 8 * J
HS = 32
NH = NP // HS
NB = 5 * D

T_LO, T_HI, T_SB, T_GB = 0, 32, 64, 96
T_LM, T_LG, T_LC, T_P, T_W, T_REL = 128, 132, 136, 140, 144, 176
T_END = T_REL + NG


def program(nc, x, src, dst, etype, eweight, weights, roots, biases, gammas, betas, out):
    h_rows = [nc.dram_tensor(f"h_rows{i}", [NP, R * D], F32, kind="Internal").ap() for i in range(2)]

    x1_rows = nc.dram_tensor("x1_rows", [P, NT * D], F32, kind="Internal").ap()

    ctx = ExitStack()
    with ctx:
        def sb(name, shape, dt=F32):
            return ctx.enter_context(nc.sbuf_tensor(name, shape, dt))

        def pb(name):
            return ctx.enter_context(nc.psum_tensor(name, [P, 512], F32))

        def sem(name):
            return ctx.enter_context(nc.semaphore(name))

        X = sb("X", [P, NT, D])
        base = sb("base", [P, NT, D])
        wts = sb("wts", [P, L, KH, NB])
        x1 = wts[:].rearrange("p l k n -> p (l k n)")[:, 0:NT * D].rearrange("p (t d) -> p t d", d=D)
        ring = sb("ring", [P, SLOTS, D])
        ringf = ring[:].rearrange("p s d -> p (s d)")
        bias_b = sb("bias_b", [P, L, D])
        gamma_b = sb("gamma_b", [P, L, D])
        beta_b = sb("beta_b", [P, L, D])
        nat_dst_i = ringf[0:NG, 0:512].bitcast(I32)
        nat_src_i = ringf[0:NG, 512:1024].bitcast(I32)
        nat_typ_i = ringf[0:NG, 1024:1536].bitcast(I32)
        nat_w = ringf[0:NG, 1536:2048]
        nat_src = ringf[0:NG, 2048:2560]
        nat_typ = ringf[0:NG, 2560:3072]
        nat_idx = ringf[0:NG, 3072:3584]
        nat_key = ringf[0:NG, 3584:4096]
        key_row = ringf[0:NG, 4096:4608]
        nat_hi_i = ringf[0:NG, 5120:5632].bitcast(I32)
        nat_lo_i = ringf[0:NG, 5632:6144].bitcast(I32)
        nat_hi = ringf[0:NG, 6144:6656]
        nat_lo = ringf[0:NG, 6656:7168]
        later = ringf[:, 4608:5120]
        src_dist = ringf[:, 0:1024].rearrange("p (j n) -> p j n", j=J)
        OS = ringf[:, 5120:5632].bitcast(BF16).rearrange("p (j n) -> p j n", j=J)
        OD = ringf[:, 5632:6656].bitcast(BF16).rearrange("p (j c n) -> p j c n", j=J, c=4)
        nat_dst = sb("nat_dst", [NG, GE])
        ecol = sb("ecol", [P, NG, 4, J])
        idx = sb("idx", [P, (NG + RG) * J], I32)
        ixb = sb("ixb", [P, 2, SLOTS], I32)
        place = sb("place", [P, NG, 2, J])
        wpart = sb("wpart", [P, NG, 3, J], BF16)
        S = sb("S", [P, J, P])
        dist = sb("dist", [P, J, P])
        hot_s = sb("hot_s", [P, 2, J, NH], BF16)
        hot_n = sb("hot_n", [P, 2, J, P], BF16)
        hot_t = sb("hot_t", [NH, 2, GE])
        Wm = sb("Wm", [P, KH, D])
        dupw = sb("dupw", [P, GE * (J + 1) // 2], BF16)
        dup = sb("dup", [P, J])
        wlast = sb("wlast", [P, 3, J], BF16)
        junk = sb("junk", [P, GE])
        ident = sb("ident", [P, P])
        ident_h = sb("ident_h", [P, P], BF16)
        ones = sb("ones", [P, P])
        iota = sb("iota", [P, D])
        iota_t = sb("iota_t", [P, P])
        tbase = sb("tbase", [P, NT])
        tri = sb("tri", [P, NT])
        grow = sb("grow", [P, NG])
        nxt_i = sb("nxt_i", [NG, 1], I32)
        nxt = sb("nxt", [NG, 1])
        cmp = sb("cmp", [NG, 64])
        bad = sb("bad", [NG, 3])
        colv = sb("colv", [NT, 16])
        rowv = sb("rowv", [1, 8])
        roww = sb("roww", [1, NT])
        relr = sb("relr", [1, NG])
        relr2 = sb("relr2", [1, NG])
        zeros = sb("zeros", [P, D], BF16)
        xcur = sb("xcur", [P, D])
        xo = sb("xo", [P, D])
        ybase = sb("ybase", [P, D])
        z2 = sb("z2", [P, D])
        z3 = sb("z3", [P, D])
        relw = sb("relw", [NT, NG])
        relx = sb("relx", [NT, NG])
        tabf = sb("tabf", [1, T_END])
        tab = sb("tab", [1, T_END], I32)
        cntm = sb("cntm", [NH, P])
        invd = sb("invd", [NH, P])
        looked = sb("looked", [P, J, P])
        y = sb("y", [P, D])
        z = sb("z", [P, D])
        zm = sb("zm", [P, D])
        ze = sb("ze", [P, D])
        xn = sb("xn", [P, D])
        xnT = sb("xnT", [P, KH, P])
        xT = sb("xT", [P, KH, P])
        hst = sb("hst", [P, R * D])
        yo = sb("yo", [P, D])
        st6 = sb("st6", [P, 6])
        mv = sb("mv", [P, 2])
        veps = sb("veps", [P, 1])
        half_bits = sb("half_bits", [P, 1], I32)
        rs = [sb(f"rs{k}", [P, 1]) for k in range(4)]
        rsv = [sb(f"rsv{k}", [P, 1]) for k in range(3)]
        rsh = [sb(f"rsh{k}", [P, 1]) for k in range(3)]

        acc = pb("acc")
        tr = pb("tr")
        hp = [pb(f"hp{i}") for i in range(3)]
        rowb = pb("rowb")
        pw = ctx.enter_context(nc.psum_tensor("pw", [P, KH, 512], F32))
        cnt_ps = acc[0:NH, 0:P]

        names = """ld_nat_a ld_nat_b ld_nxt ld_x ld_w ld_par nat_zero ground made nat_conv nat_join nat_split col_tr col_out
                   tb_cmp tb_cols tb_rows tb_table tab_ready
                   wm_zero key_masked key_row_ready w_split w_src_dist w_src_hot w_ready w_dup w_last w_dst_hot w_hot w_mm w_upd
                   xcur_ready x_tr xT_ready x_mm
                   hot_ready cnt_mm cnt_max inv_ready hot_tr hot_t_ready inv_mm inv_found inv_all
                   iota_ready S_dist S_ready agg_mm idx_copied tiles_landed passed
                   y_based y_ready n_stats n_mv n_newton n_gamma n_beta n_min n_exp n_elu
                   xn_ready xn_stored xn_tr xnT_ready h_mm h_out h_stored
                   x1_saved x1_back f_sum f_stats f_mv f_newton f_norm out_stored""".split()
        s = {n: sem(n) for n in names}
        landed = [sem(f"landed{k}") for k in range(SLOTS)]

        block = ctx.enter_context(nc.Block())

        MAXS = NT * NG * L

        def entry(eng, col, lo, hi):
            return eng.value_load(tab[0:1, bass.ds(col, 1)], min_val=lo, max_val=hi)

        def tile_bounds(eng, t):
            return entry(eng, t + T_LO, 0, NG - 2), entry(eng, t + T_HI, 2, NG), entry(eng, t + T_SB, 0, MAXS)

        @block.sync
        def _(sp):
            sp.wait_ge(s["nat_zero"], 5)
            full, rest = (NG - 1) * GE, E - (NG - 1) * GE
            for a, b in ((dst, nat_dst_i), (src, nat_src_i), (etype, nat_typ_i), (eweight, nat_w)):
                sp.dma_start(b[0:NG - 1, :], a[0:full].rearrange("(g e) -> g e", e=GE)).then_inc(s["ld_nat_a"], 16)
                sp.dma_start(b[NG - 1:NG, 0:rest], a[full:E].rearrange("(g e) -> g e", e=rest)).then_inc(s["ld_nat_b"], 16)
            sp.dma_start(nxt_i[0:NG - 2, :], dst[GE:full].rearrange("(g e) -> g e", e=GE)[:, 0:1],
                         allow_slow_non_contiguous=True).then_inc(s["ld_nxt"], 16)
            sp.dma_start(nxt_i[NG - 2:NG - 1, :], dst[full:full + 1].rearrange("(g e) -> g e", e=1)).then_inc(s["ld_nxt"], 16)
            sp.dma_start(X[:, 0:NT - 1, :], x[0:(NT - 1) * P, :].rearrange("(t p) d -> p t d", p=P)).then_inc(s["ld_x"], 16)
            sp.dma_start(X[0:N - (NT - 1) * P, NT - 1, :], x[(NT - 1) * P:N, :]).then_inc(s["ld_x"], 16)
            for l in range(L):
                for k in range(KH):
                    for r in range(R):
                        sp.dma_start(wts[:, l, k, r * D:(r + 1) * D], weights[l, r, k * P:(k + 1) * P, :]).then_inc(s["ld_w"], 16)
                    sp.dma_start(wts[:, l, k, R * D:NB], roots[l, k * P:(k + 1) * P, :]).then_inc(s["ld_w"], 16)
            for a, b in ((biases, bias_b), (gammas, gamma_b), (betas, beta_b)):
                sp.dma_start(b[:], a.rearrange("(o l) d -> o l d", o=1).to_broadcast([P, L, D])).then_inc(s["ld_par"], 16)

            sp.wait_ge(s["tab_ready"], 1)
            passes = entry(sp, T_P, 1, NT)
            with sp.Fori(0, L) as l:
                lc = entry(sp, l + T_LC, 0, L * NT * CYC)
                with sp.Fori(0, passes) as p:
                    with sp.Fori(0, CYC) as c:
                        for k in range(SLOTS):
                            sp.wait_ge(landed[k], (lc + p * CYC + c + 1) * 16)
                            sp.sem_inc(s["tiles_landed"], 1)

        @block.gpsimd
        def _(pool):
            pool.memset(nat_dst_i, NP).then_inc(s["nat_zero"], 1)
            pool.memset(nat_src_i, 0).then_inc(s["nat_zero"], 1)
            pool.memset(nat_typ_i, 0).then_inc(s["nat_zero"], 1)
            pool.memset(nat_w, 0.0).then_inc(s["nat_zero"], 1)
            pool.memset(X[:, NT - 1, :], 0.0)
            pool.memset(nxt_i[:], NP).then_inc(s["nat_zero"], 1)
            pool.memset(ident[:], 0.0)
            pool.memset(ones[:], 1.0)
            pool.memset(later, 1.0)
            pool.memset(tri[:], 0.0)
            pool.memset(zeros[:], 0.0)
            pool.iota(iota[:], [[1, D]], base=0, channel_multiplier=0, allow_small_or_imprecise_dtypes=True)
            pool.iota(tbase[:], [[P, NT]], base=0, channel_multiplier=0, allow_small_or_imprecise_dtypes=True)
            pool.iota(grow[:], [[1, NG]], base=1 - RG, channel_multiplier=0, allow_small_or_imprecise_dtypes=True).then_inc(s["ground"], 1)
            pool.wait_ge(s["ground"], 1)
            pool.affine_select(out=ident[:], in_=ident[:], compare_op=ALU.not_equal, fill=1.0, base=0,
                               pattern=[[-1, P]], channel_multiplier=1)
            pool.affine_select(out=later, in_=later, compare_op=ALU.is_gt, fill=0.0, base=0,
                               pattern=[[1, GE]], channel_multiplier=-1)
            pool.affine_select(out=tri[:], in_=tri[:], compare_op=ALU.is_ge, fill=1.0, base=0,
                               pattern=[[-1, NT]], channel_multiplier=1).then_inc(s["made"], 1)

            pool.wait_ge(s["w_mm"], 2)
            pool.wait_ge(s["w_ready"], 1)
            passes = entry(pool, T_P, 1, NT)
            def gathers(l, h_gather):
                pool.wait_ge(s["h_stored"], (l + 1) * (16 * NT))
                pool.sem_inc(s["passed"], 1)
                lm = entry(pool, l + T_LM, 0, MAXS)
                lc = entry(pool, l + T_LC, 0, L * NT * CYC)
                with pool.Fori(0, passes) as p:
                    with pool.Fori(0, CYC // 2) as c2:
                        for b in range(2):
                            c = c2 * 2 + b
                            q = lc + p * CYC + c
                            pool.wait_ge(s["idx_copied"], q + 1)
                            for g in range(RG):
                                rel = entry(pool, c * RG + (T_REL + g), 1, MAXS * J)
                                pool.wait_ge(s["agg_mm"], (lm + p * NG) * J + rel)
                                pool.sem_inc(s["passed"], 1)
                                if g == RG - 1:
                                    pool.tensor_copy(ixb[:, 1 - b, :], idx[:, bass.ds(c * SLOTS + SLOTS, SLOTS)]).then_inc(s["idx_copied"], 1)
                                for j in range(J):
                                    k = g * J + j
                                    pool.indirect_dma_start(ring[:, k, :], None, h_gather,
                                                            bass.IndirectOffsetOnAxis(ap=ixb[:, b, k:k + 1], axis=0)).then_inc(landed[k], 16)

            pool.tensor_copy(ixb[:, 0, :], idx[:, 0:SLOTS]).then_inc(s["idx_copied"], 1)
            with pool.Fori(0, L // 2) as two:
                for half in range(2):
                    gathers(two * 2 + half, h_rows[half].rearrange("n (r d) -> (n r) d", r=R))

        @block.tensor
        def _(pe):
            pe.sem_inc(s["agg_mm"], BIAS)
            pe.sem_inc(s["w_src_hot"], J)
            pe.sem_inc(s["w_mm"], 1)
            pe.sem_inc(s["w_upd"], 2)
            for n in ("cnt_mm", "hot_tr", "hot_t_ready", "inv_mm", "inv_found"):
                pe.sem_inc(s[n], 2)
            pe.sem_inc(s["S_ready"], J)
            pe.sem_inc(s["tiles_landed"], J)
            pe.wait_ge(s["made"], 1)

            pe.wait_ge(s["nat_join"], 4)
            for a, arr in enumerate((nat_dst[:], nat_src, nat_key, nat_w, nat_idx, nat_hi, nat_lo)):
                bank = (tr, rowb)[a % 2]
                if a >= 2:
                    pe.wait_ge(s["col_out"], a - 1)
                for j in range(J):
                    m = nc.tensor.transpose(bank[:, j * P:j * P + NG], arr[:, j * P:(j + 1) * P], ident[0:NG, 0:NG])
                m.then_inc(s["col_tr"], 1)

            pe.wait_ge(s["tb_cmp"], 6)
            nc.tensor.matmul(acc[0:NT, 0:1], cmp[:, 0:NT], ones[0:NG, 0:1], start=True, stop=True)
            nc.tensor.matmul(acc[0:NT, 8:9], cmp[:, 32:32 + NT], ones[0:NG, 0:1], start=True, stop=True)
            nc.tensor.matmul(acc[0:NT, 16:17], ones[0:NG, 0:NT], bad[:, 2:3], start=True, stop=True).then_inc(s["tb_rows"], 1)
            pe.wait_ge(s["tb_cols"], 16)
            nc.tensor.matmul(acc[0:1, 32:32 + NT], colv[:, 6:7], ident[0:NT, 0:NT], start=True, stop=True)
            nc.tensor.matmul(acc[0:1, 64:64 + NT], colv[:, 8:9], ident[0:NT, 0:NT], start=True, stop=True)
            nc.tensor.matmul(acc[0:1, 96:96 + NT], colv[:, 9:10], tri[0:NT, :], start=True, stop=False)
            nc.tensor.matmul(acc[0:1, 96:96 + NT], colv[:, 10:11], ident[0:NT, 0:NT], start=False, stop=True)
            nc.tensor.matmul(acc[0:1, 128:129], colv[:, 9:10], ones[0:NT, 0:1], start=True, stop=True)
            nc.tensor.matmul(acc[0:1, 132:133], colv[0:1, 3:4], ones[0:1, 0:1], start=True, stop=True)
            nc.tensor.matmul(acc[0:1, 160:160 + NG], ones[0:NT, 0:1], relx[:], start=True, stop=True).then_inc(s["tb_rows"], 1)

            pe.wait_ge(s["tab_ready"], 1)
            pe.wait_ge(s["w_split"], 5)

            def key_row_out(q):
                pe.wait_ge(s["key_masked"], q + 1)
                nc.tensor.matmul(rowb[:], ones[0:NG, :], key_row, start=True, stop=True).then_inc(s["key_row_ready"], 1)

            for t in range(KH):
                lo_t, end_t, sb_t = tile_bounds(pe, t)
                key_row_out(sb_t + lo_t + t)
                with pe.Fori(lo_t, end_t) as g:
                    w = sb_t + g
                    pe.wait_ge(s["w_dup"], w * J + J)
                    key_row_out(w + (t + 1))
                    pe.wait_ge(s["w_src_hot"], w * J + 2 * J)
                    pe.wait_ge(s["w_upd"], w * 2 + 2)
                    for c in range(3):
                        pe.wait_ge(s["w_hot"], w * 3 + (c + 1))
                        for j in range(J):
                            for k in range(KH):
                                rhs = OD[:, j, 0:2, :].rearrange("p c n -> p (c n)") if c == 0 else OD[:, j, c + 1, :]
                                m = nc.tensor.matmul(pw[:, k, 0 if c == 0 else P:2 * P], OS[:, j, k * P:(k + 1) * P], rhs,
                                                     start=j == 0 and c == 0, stop=j == J - 1, skip_group_check=True)
                    m.then_inc(s["w_mm"], 1)

            def turn(e):
                pe.wait_ge(s["xn_ready"], e + 1)
                for k in range(KH):
                    m = nc.tensor.transpose(tr[:, k * P:(k + 1) * P], xn[:, k * P:(k + 1) * P], ident[:])
                m.then_inc(s["xn_tr"], 1)

            def node_products(e, layer, first=False):
                if not first:
                    pe.wait_ge(s["h_out"], e * 3)
                pe.wait_ge(s["xnT_ready"], e + 1)
                for b, (c0, c1) in enumerate(((0, 512), (512, 1024), (1024, NB))):
                    for k in range(KH):
                        rhs = wts[:, bass.ds(layer, 1), k, c0:c1].rearrange("p a c -> p (a c)")
                        m = nc.tensor.matmul(hp[b][:, 0:c1 - c0], xnT[:, k, :], rhs, start=k == 0, stop=k == KH - 1)
                    m.then_inc(s["h_mm"], 1)

            def turn_x(t):
                pe.wait_ge(s["xcur_ready"], t + 1)
                for k in range(KH):
                    m = nc.tensor.transpose(rowb[:, k * P:(k + 1) * P], xcur[:, k * P:(k + 1) * P], ident[:])
                m.then_inc(s["x_tr"], 1)

            def first_product(t, first=False):
                if not first:
                    pe.wait_ge(s["y_ready"], t)
                pe.wait_ge(s["xT_ready"], t + 1)
                for k in range(KH):
                    m = nc.tensor.matmul(acc[:, 0:D], xT[:, k, :], Wm[:, k, :], start=k == 0, stop=k == KH - 1)
                m.then_inc(s["x_mm"], 1)

            pe.wait_ge(s["w_ready"], 1)
            turn_x(0)
            first_product(0, first=True)
            turn_x(1)
            pe.wait_ge(s["ld_w"], 16 * L * KH * (R + 1))
            first_product(1)
            turn(0)
            turn_x(2)
            node_products(0, 0, first=True)
            with pe.Fori(2, NT - 1) as t:
                first_product(t)
                turn(t - 1)
                turn_x(t + 1)
                node_products(t - 1, 0)
            first_product(NT - 1)
            turn(NT - 2)
            node_products(NT - 2, 0)
            turn(NT - 1)
            node_products(NT - 1, 0)

            pe.wait_ge(s["y_ready"], NT)
            nc.tensor.matmul(cnt_ps, zeros[:, 0:NH], zeros[:, 0:P], start=True, stop=True)
            with pe.Fori(0, NG // 2) as two:
                for half in range(2):
                    g = two * 2 + half
                    pe.wait_ge(s["hot_ready"], g + 1)
                    for j in range(J):
                        m = nc.tensor.matmul(cnt_ps, hot_s[:, half, j, :], hot_n[:, half, j, :],
                                             start=False, stop=True, skip_group_check=True)
                    m.then_inc(s["cnt_mm"], 1)

            def turn_hot(g, half):
                pe.wait_ge(s["hot_ready"], g + (NG + 1))
                pe.wait_ge(s["hot_t_ready"], g + 1)
                for j in range(J):
                    m = nc.tensor.transpose((rowb, tr)[half][:].bitcast(BF16)[0:NH, j * P:(j + 1) * P], hot_s[:, half, j, :], ident_h[:])
                m.then_inc(s["hot_tr"], 1)

            def look_up(g, half):
                pe.wait_ge(s["hot_t_ready"], g + 3)
                pe.wait_ge(s["inv_found"], g + 1)
                for j in range(J):
                    m = nc.tensor.matmul(hp[half][:, j * P:(j + 1) * P], hot_t[:, half, j * P:(j + 1) * P], invd[:], start=True, stop=True)
                m.then_inc(s["inv_mm"], 1)

            pe.wait_ge(s["inv_ready"], 1)
            pe.wait_ge(s["h_out"], 3 * NT)
            turn_hot(0, 0)
            with pe.Fori(0, NG // 2 - 1) as two:
                for half in range(2):
                    g = two * 2 + half
                    turn_hot(g + 1, 1 - half)
                    look_up(g, half)
            turn_hot(NG - 1, 1)
            look_up(NG - 2, 0)
            look_up(NG - 1, 1)

            def aggregate(l, t, lm, lg, before_last=None):
                lo_t, end_t, sb_t = tile_bounds(pe, t)
                gb_t = entry(pe, t + T_GB, 0, MAXS * J)
                pe.wait_ge(s["y_ready"], l * NT + (t + NT))
                nc.tensor.matmul(acc[:, 0:D], zeros[:, 0:P], zeros[:], start=True, stop=True)

                def group(g, after):
                    for j in range(J):
                        pe.wait_ge(s["S_ready"], (lm + sb_t + after) * J + (j + 1))
                        pe.wait_ge(s["tiles_landed"], lg + gb_t + after * J + (j + 1))
                        nc.tensor.matmul(acc[:, 0:D], S[:, j, :],
                                         ring[:, bass.ds(g % RG * J + j, 1), :].rearrange("p a d -> p (a d)"),
                                         start=False, stop=True, skip_group_check=True).then_inc(s["agg_mm"], 1)

                with pe.Fori(lo_t, end_t - 1) as g:
                    group(g, g + 1)
                if before_last is not None:
                    before_last()
                group(end_t - 1, end_t)

            with pe.Fori(0, L - 1) as l:
                lm = entry(pe, l + T_LM, 0, MAXS)
                lg = entry(pe, l + T_LG, 0, MAXS * J)
                aggregate(l, 0, lm, lg)
                with pe.Fori(1, NT) as t:
                    aggregate(l, t, lm, lg, lambda: turn(l * NT + (t + NT - 1)))
                    node_products(l * NT + (t + NT - 1), l + 1)
                turn(l * NT + (2 * NT - 1))
                node_products(l * NT + (2 * NT - 1), l + 1)
            lm = entry(pe, T_LM + L - 1, 0, MAXS)
            lg = entry(pe, T_LG + L - 1, 0, MAXS * J)
            with pe.Fori(0, NT) as t:
                aggregate(L - 1, t, lm, lg)

        @block.scalar
        def _(act):
            def transposed(e, first=False):
                act.wait_ge(s["xn_tr"], e + 1)
                if not first:
                    act.wait_ge(s["h_mm"], e * 3)
                nc.scalar.activation(xnT[:].rearrange("p k n -> p (k n)"), tr[:, 0:D], ACT.Copy).then_inc(s["xnT_ready"], 1)

            def store_messages(e, t, half):
                act.wait_ge(s["h_out"], e * 3 + 2)
                act.dma_start(h_rows[half][bass.ds(t * P, P), :], hst[:]).then_inc(s["h_stored"], 16)

            def products_out(e, t, half, first=False):
                act.wait_ge(s["h_mm"], e * 3 + 1)
                if not first:
                    act.wait_ge(s["h_stored"], e * 16)
                nc.scalar.activation(hst[:, 0:512], hp[0][:], ACT.Copy).then_inc(s["h_out"], 1)
                act.wait_ge(s["h_mm"], e * 3 + 2)
                nc.scalar.activation(hst[:, 512:1024], hp[1][:], ACT.Copy).then_inc(s["h_out"], 1)
                act.wait_ge(s["h_mm"], e * 3 + 3)
                act.sem_inc(s["passed"], 1)
                nc.scalar.activation(base[:, bass.ds(t, 1), :].rearrange("p a d -> p (a d)"), hp[2][:, 0:D],
                                     ACT.Copy).then_inc(s["h_out"], 1)
                store_messages(e, t, half)

            def store_xn(e, t):
                act.wait_ge(s["xn_ready"], e + 1)
                act.sem_inc(s["passed"], 1)
                nc.scalar.activation(X[:, bass.ds(t, 1), :].rearrange("p a d -> p (a d)"), xn[:], ACT.Copy).then_inc(s["xn_stored"], 1)

            def current_x(t, first=False):
                if not first:
                    act.wait_ge(s["x_tr"], t)
                    act.sem_inc(s["passed"], 1)
                nc.scalar.activation(xcur[:], X[:, bass.ds(t, 1), :].rearrange("p a d -> p (a d)"), ACT.Copy).then_inc(s["xcur_ready"], 1)

            def x_transposed(t, first=False):
                act.wait_ge(s["x_tr"], t + 1)
                if not first:
                    act.wait_ge(s["x_mm"], t)
                nc.scalar.activation(xT[:].rearrange("p k n -> p (k n)"), rowb[:, 0:D], ACT.Copy).then_inc(s["xT_ready"], 1)

            act.wait_ge(s["tab_ready"], 1)
            nc.scalar.activation(xcur[:, 0:1], iota[:, 0:1], ACT.Abs)
            for t in range(KH):
                lo_t, end_t, sb_t = tile_bounds(act, t)
                with act.Fori(lo_t, end_t) as g:
                    w = sb_t + g
                    act.wait_ge(s["w_src_hot"], w * J + J)
                    act.sem_inc(s["passed"], 1)
                    for j in range(J):
                        nc.scalar.activation(src_dist[:, j, :], iota[:], ACT.Abs, scale=-1.0,
                                             bias=ecol[:, bass.ds(g, 1), 1, j:j + 1].rearrange("p a j -> p (a j)")).then_inc(s["w_src_dist"], 1)
                    act.wait_ge(s["w_mm"], w + 1)
                    for j in range(J):
                        act.wait_ge(s["w_src_dist"], w * J + (j + 1))
                        nc.scalar.activation(OS[:, j, :], src_dist[:, j, :], ACT.Relu, bias=ones[:, 0:1], scale=-1.0).then_inc(s["w_src_hot"], 1)

            act.wait_ge(s["ld_x"], 32)
            act.wait_ge(s["w_ready"], 1)
            current_x(0, first=True)
            x_transposed(0, first=True)
            current_x(1)
            x_transposed(1)
            current_x(2)
            store_xn(0, 0)
            transposed(0, first=True)
            x_transposed(2)
            current_x(3)
            store_xn(1, 1)
            products_out(0, 0, 0, first=True)
            with act.Fori(2, NT - 2) as t:
                transposed(t - 1)
                x_transposed(t + 1)
                current_x(t + 2)
                store_xn(t, t)
                products_out(t - 1, t - 1, 0)
            transposed(NT - 3)
            x_transposed(NT - 1)
            store_xn(NT - 2, NT - 2)
            products_out(NT - 3, NT - 3, 0)
            transposed(NT - 2)
            store_xn(NT - 1, NT - 1)
            products_out(NT - 2, NT - 2, 0)
            transposed(NT - 1)
            products_out(NT - 1, NT - 1, 0)

            act.wait_ge(s["xn_stored"], NT)
            act.dma_start(x1_rows, X[:].rearrange("p t d -> p (t d)")).then_inc(s["x1_saved"], 16)
            act.wait_ge(s["x1_saved"], 16)
            act.sem_inc(s["passed"], 1)

            with act.Fori(0, NG // 2) as two:
                for half in range(2):
                    g = two * 2 + half
                    act.wait_ge(s["hot_tr"], g + 3)
                    act.wait_ge(s["inv_mm"], g + 1)
                    nc.scalar.activation(hot_t[:, half, :], (rowb, tr)[half][:].bitcast(BF16)[0:NH, 0:GE], ACT.Copy).then_inc(s["hot_t_ready"], 1)

            def elu_exp(el):
                act.wait_ge(s["n_min"], el + 1)
                nc.scalar.activation(ze[:], zm[:], ACT.Exp).then_inc(s["n_exp"], 1)

            def node_numbers(l, t, bounds, lm):
                act.wait_ge(s["S_ready"], (lm + bounds[2] + bounds[0]) * J + J)
                act.sem_inc(s["passed"], 1)
                nc.scalar.activation(iota_t[:], iota[:, 0:P], ACT.Identity, bias=tbase[:, bass.ds(t, 1)]).then_inc(s["iota_ready"], 1)
                act.wait_ge(s["iota_ready"], l * NT + (t + 1))
                act.sem_inc(s["passed"], 1)

            def weigh(g, w):
                def column(a, j):
                    return ecol[:, bass.ds(g, 1), a, j:j + 1].rearrange("p a j -> p (a j)")
                act.wait_ge(s["S_ready"], w * J + J)
                act.sem_inc(s["passed"], 1)
                for j in range(J):
                    nc.scalar.activation(dist[:, j, :], iota_t[:], ACT.Abs, bias=column(0, j), scale=-1.0).then_inc(s["S_dist"], 1)
                for j in range(J):
                    act.wait_ge(s["S_dist"], w * J + (j + 1))
                    act.wait_ge(s["agg_mm"], w * J + (j + 1 + BIAS - J))
                    act.sem_inc(s["passed"], 1)
                    nc.scalar.activation(S[:, j, :], dist[:, j, :], ACT.Relu, bias=column(1, j), scale=column(2, j)).then_inc(s["S_ready"], 1)

            def weigh_first(l, t, bounds, lm):
                node_numbers(l, t, bounds, lm)
                weigh(bounds[0], lm + bounds[2] + bounds[0])

            def weigh_rest(bounds, lm):
                lo_t, end_t, sb_t = bounds
                with act.Fori(lo_t + 1, end_t) as g:
                    weigh(g, lm + sb_t + g)

            act.wait_ge(s["inv_all"], 1)
            act.sem_inc(s["passed"], 1)
            for l in range(L - 1):
                half = (l + 1) % 2
                lm = entry(act, T_LM + l, 0, MAXS)
                bounds = tile_bounds(act, 0)
                weigh_first(l, 0, bounds, lm)
                weigh_rest(bounds, lm)

                def step(t, first=False):
                    bounds = tile_bounds(act, t)
                    weigh_first(l, t, bounds, lm)
                    elu_exp(l * NT + (t - 1))
                    weigh_rest(bounds, lm)
                    if not first:
                        store_messages(l * NT + (t + NT - 2), t - 2, half)

                step(1, first=True)
                with act.Fori(2, NT) as t:
                    step(t)
                elu_exp(l * NT + (NT - 1))
                store_messages(l * NT + (2 * NT - 2), NT - 2, half)
                store_messages(l * NT + (2 * NT - 1), NT - 1, half)

            act.wait_ge(s["h_mm"], L * NT * 3)
            act.dma_start(x1.rearrange("p t d -> p (t d)"), x1_rows).then_inc(s["x1_back"], 16)

            def store_out(t):
                act.wait_ge(s["f_norm"], t + 1)
                act.dma_start(out[bass.ds(t * P, P), :], yo[:]).then_inc(s["out_stored"], 16)

            def last_step(t, first=False):
                bounds = tile_bounds(act, t)
                weigh_first(L - 1, t, bounds, lm)
                if not first:
                    store_out(t - 2)
                elu_exp((L - 1) * NT + (t - 1))
                weigh_rest(bounds, lm)

            lm = entry(act, T_LM + L - 1, 0, MAXS)
            bounds = tile_bounds(act, 0)
            weigh_first(L - 1, 0, bounds, lm)
            weigh_rest(bounds, lm)
            last_step(1, first=True)
            with act.Fori(2, NT) as t:
                last_step(t)
            store_out(NT - 2)
            elu_exp(L * NT - 1)
            act.wait_ge(s["f_norm"], NT)
            act.dma_start(out[(NT - 1) * P:N, :], yo[0:N - (NT - 1) * P, :]).then_inc(s["out_stored"], 16)
            act.wait_ge(s["out_stored"], 16 * NT)

        @block.vector
        def _(dve):
            v = nc.vector
            dve.wait_ge(s["ld_nat_a"], 16 * 4)
            dve.wait_ge(s["ld_nat_b"], 16 * 4)
            v.tensor_copy(nat_dst[:], nat_dst_i)
            v.tensor_copy(nat_src, nat_src_i)
            v.tensor_copy(nat_typ, nat_typ_i).then_inc(s["nat_conv"], 1)
            dve.wait_ge(s["nat_conv"], 1)
            v.scalar_tensor_tensor(out=nat_key, in0=nat_src, scalar=float(KEY), in1=nat_dst[:], op0=ALU.mult, op1=ALU.add).then_inc(s["nat_join"], 1)
            v.scalar_tensor_tensor(out=nat_idx, in0=nat_src, scalar=float(R), in1=nat_typ, op0=ALU.mult, op1=ALU.add).then_inc(s["nat_join"], 1)

            v.tensor_scalar(nat_hi_i, nat_dst_i, HS.bit_length() - 1, None, ALU.logical_shift_right).then_inc(s["nat_split"], 1)
            v.tensor_scalar(nat_lo_i, nat_dst_i, HS - 1, None, ALU.bitwise_and).then_inc(s["nat_split"], 1)
            dve.wait_ge(s["nat_split"], 2)
            v.tensor_copy(nat_hi, nat_hi_i).then_inc(s["nat_join"], 1)
            v.scalar_tensor_tensor(out=nat_lo, in0=nat_lo_i, scalar=float(R), in1=nat_typ, op0=ALU.mult, op1=ALU.add).then_inc(s["nat_join"], 1)

            dve.wait_ge(s["made"], 1)
            dve.wait_ge(s["ld_nxt"], 32)
            v.tensor_scalar(cmp[:, 0:NT], tbase[0:NG, :], nat_dst[:, 0:1], float(-P), ALU.subtract, ALU.is_gt).then_inc(s["tb_cmp"], 1)
            v.tensor_scalar(cmp[:, 32:32 + NT], tbase[0:NG, :], nat_dst[:, GE - 1:GE], 0.0, ALU.subtract, ALU.is_gt).then_inc(s["tb_cmp"], 1)
            v.tensor_tensor(junk[0:NG, 0:GE - 1], nat_dst[:, 1:GE], nat_dst[:, 0:GE - 1], ALU.is_lt)
            v.tensor_copy(nxt[:], nxt_i[:]).then_inc(s["tb_cmp"], 1)
            dve.wait_ge(s["tb_cmp"], 3)
            v.tensor_reduce(bad[:, 0:1], junk[0:NG, 0:GE - 1], AX.X, ALU.max).then_inc(s["tb_cmp"], 1)
            v.tensor_tensor(bad[:, 1:2], nxt[:], nat_dst[:, GE - 1:GE], ALU.is_lt).then_inc(s["tb_cmp"], 1)
            dve.wait_ge(s["tb_cmp"], 5)
            v.tensor_tensor(bad[:, 2:3], bad[:, 0:1], bad[:, 1:2], ALU.max).then_inc(s["tb_cmp"], 1)

            dup_at = [sum(GE - k * P for k in range(j)) for j in range(J + 1)]

            def columns(a, out_ap, bank):
                dve.wait_ge(s["col_tr"], a + 1)
                return v.tensor_scalar(out_ap, bank[:].rearrange("p (j g) -> p j g", j=J)[:, :, 0:NG].rearrange("p j g -> p g j"),
                                       0.0, None, ALU.add)
            for a in range(4):
                columns(a, ecol[:, :, a, :], (tr, rowb)[a % 2]).then_inc(s["col_out"], 1)
            columns(4, idx[:, 0:NG * J].rearrange("p (g j) -> p g j", j=J), tr).then_inc(s["col_out"], 1)
            dve.wait_ge(s["col_out"], 5)
            v.tensor_copy(idx[:, NG * J:(NG + RG) * J], idx[:, 0:SLOTS])
            for a in range(2):
                columns(5 + a, place[:, :, a, :], (rowb, tr)[a]).then_inc(s["col_out"], 1)

            c = lambda n: colv[:, n:n + 1]
            step = [0]

            def col(ins):
                step[0] += 1
                ins.then_inc(s["tb_cols"], 1)
                dve.wait_ge(s["tb_cols"], step[0])
            dve.wait_ge(s["tb_rows"], 1)
            col(v.tensor_scalar(c(3), acc[0:NT, 16:17], 1.0, None, ALU.min))
            col(v.tensor_scalar(c(4), c(3), -1.0, 1.0, ALU.mult, ALU.add))
            col(v.tensor_scalar(c(1), acc[0:NT, 0:1], 1.0, None, ALU.max))
            col(v.tensor_scalar(c(5), c(1), 1.0, None, ALU.subtract))
            col(v.tensor_tensor(c(0), acc[0:NT, 8:9], c(5), ALU.min))
            col(v.tensor_tensor(c(2), c(0), c(4), ALU.mult))
            col(v.tensor_scalar(c(6), c(2), float(NG - 2), None, ALU.min))
            col(v.tensor_tensor(c(7), c(1), c(4), ALU.mult))
            col(v.scalar_tensor_tensor(out=c(11), in0=c(3), scalar=float(NG), in1=c(7), op0=ALU.mult, op1=ALU.add))
            col(v.scalar_tensor_tensor(out=c(8), in0=c(6), scalar=2.0, in1=c(11), op0=ALU.add, op1=ALU.max))
            col(v.tensor_tensor(c(9), c(8), c(6), ALU.subtract))
            col(v.tensor_scalar(c(10), c(6), -1.0, None, ALU.mult))
            col(v.tensor_scalar(c(12), c(8), 1.0, None, ALU.subtract))
            col(v.tensor_scalar(c(13), c(6), 1.0, None, ALU.subtract))
            col(v.tensor_scalar(relw[:], grow[0:NT, :], c(12), c(13), ALU.min, ALU.subtract))
            col(v.tensor_scalar(relx[:], relw[:], 0.0, None, ALU.max))

            r_ = lambda n: rowv[:, n:n + 1]
            count = [0]

            def row(ins):
                count[0] += 1
                ins.then_inc(s["tb_table"], 1)
                dve.wait_ge(s["tb_table"], count[0])
            dve.wait_ge(s["tb_rows"], 2)
            row(v.memset(tabf[:], 0.0))
            row(v.tensor_scalar(r_(0), acc[0:1, 128:129], 0.0, None, ALU.add))
            row(v.tensor_scalar(r_(1), acc[0:1, 132:133], 0.0, None, ALU.add))
            row(v.tensor_scalar(r_(2), r_(1), -1.0, 1.0, ALU.mult, ALU.add))
            row(v.tensor_scalar(r_(3), r_(1), float(NT - 1), 1.0, ALU.mult, ALU.add))
            v.tensor_scalar(tabf[:, T_P:T_P + 1], r_(3), 0.0, None, ALU.add)
            v.tensor_scalar(tabf[:, T_LO:T_LO + NT], acc[0:1, 32:32 + NT], 0.0, None, ALU.add)
            v.tensor_scalar(tabf[:, T_HI:T_HI + NT], acc[0:1, 64:64 + NT], 0.0, None, ALU.add)
            v.tensor_scalar(tabf[:, T_SB:T_SB + NT], acc[0:1, 96:96 + NT], 0.0, None, ALU.add)
            row(v.tensor_scalar(roww[:], acc[0:1, 96:96 + NT], 0.0, None, ALU.add))
            v.tensor_tensor(tabf[:, T_W:T_W + NT], roww[:], acc[0:1, 32:32 + NT], ALU.add)
            v.tensor_scalar(tabf[:, T_GB:T_GB + NT], tbase[0:1, :], r_(1), float(NG * J) / P, ALU.mult, ALU.mult)
            v.tensor_scalar(tabf[:, T_LM:T_LM + L], iota[0:1, 0:L], r_(0), None, ALU.mult)
            v.tensor_scalar(tabf[:, T_LG:T_LG + L], iota[0:1, 0:L], r_(3), float(NG * J), ALU.mult, ALU.mult)
            v.tensor_scalar(tabf[:, T_LC:T_LC + L], iota[0:1, 0:L], r_(3), float(CYC), ALU.mult, ALU.mult)
            row(v.tensor_scalar(relr[:], acc[0:1, 160:160 + NG], r_(2), None, ALU.mult))
            row(v.scalar_tensor_tensor(out=relr2[:], in0=grow[0:1, :], scalar=r_(1), in1=relr[:], op0=ALU.mult, op1=ALU.add))
            row(v.tensor_scalar(tabf[:, T_REL:T_END], relr2[:], float(J), float(BIAS), ALU.mult, ALU.add))
            v.tensor_copy(ident_h[:], ident[:])
            v.memset(Wm[:], 0.0).then_inc(s["wm_zero"], 1)
            v.tensor_copy(tab[:], tabf[:]).then_inc(s["tab_ready"], 1)
            dve.wait_ge(s["tab_ready"], 1)
            dve.wait_ge(s["wm_zero"], 1)

            split = s["w_split"]
            w_all = ecol[:, :, 3, :]
            rest = [a[:].rearrange("p j n -> p (j n)")[:, 0:NG * J].rearrange("p (g j) -> p g j", j=J) for a in (S, dist)]
            v.tensor_copy(wpart[:, :, 0, :], w_all).then_inc(split, 1)
            dve.wait_ge(split, 1)
            v.tensor_tensor(rest[0], w_all, wpart[:, :, 0, :], ALU.subtract).then_inc(split, 1)
            dve.wait_ge(split, 2)
            v.tensor_copy(wpart[:, :, 1, :], rest[0]).then_inc(split, 1)
            dve.wait_ge(split, 3)
            v.tensor_tensor(rest[1], rest[0], wpart[:, :, 1, :], ALU.subtract).then_inc(split, 1)
            dve.wait_ge(split, 4)
            v.tensor_copy(wpart[:, :, 2, :], rest[1]).then_inc(split, 1)
            dve.wait_ge(split, 5)

            def mask_keys(g):
                v.tensor_scalar(key_row, nat_key, ident[0:NG, bass.ds(g, 1)], None, ALU.mult).then_inc(s["key_masked"], 1)

            for t in range(KH):
                lo_t, end_t, sb_t = tile_bounds(dve, t)
                Wt = Wm[:, :, t * P:(t + 1) * P]

                def same_keys(g, w):
                    dve.wait_ge(s["key_row_ready"], w + (t + 1))
                    for j in range(J):
                        v.scalar_tensor_tensor(out=dupw[:, dup_at[j]:dup_at[j + 1]], in0=rowb[:, j * P:GE],
                                               scalar=ecol[:, bass.ds(g, 1), 2, j:j + 1].rearrange("p a j -> p (a j)"),
                                               in1=later[:, 0:GE - j * P], op0=ALU.is_equal, op1=ALU.mult,
                                               accum_out=dup[:, j:j + 1]).then_inc(s["w_dup"], 1)
                    mask_keys(g + 1)

                def dst_hots(g, w):
                    v.tensor_tensor(OD[:, :, 0, :], iota[:, t * P:(t + 1) * P].unsqueeze(1).to_broadcast([P, J, P]),
                                    ecol[:, bass.ds(g, 1), 0, :].rearrange("p a j -> p (a j)").unsqueeze(2).to_broadcast([P, J, P]),
                                    ALU.is_equal).then_inc(s["w_dst_hot"], 1)
                    dve.wait_ge(s["w_dup"], w * J + J)
                    v.scalar_tensor_tensor(out=wlast[:], in0=dup[:].unsqueeze(1).to_broadcast([P, 3, J]), scalar=0.0,
                                           in1=wpart[:, bass.ds(g, 1), :, :].rearrange("p a c j -> p (a c) j"), op0=ALU.is_equal,
                                           op1=ALU.mult).then_inc(s["w_last"], 1)
                    dve.wait_ge(s["w_dst_hot"], w + 1)
                    dve.wait_ge(s["w_last"], w + 1)
                    for c in range(3):
                        v.tensor_tensor(OD[:, :, c + 1, :], OD[:, :, 0, :], wlast[:, c, :].unsqueeze(2).to_broadcast([P, J, P]),
                                        ALU.mult).then_inc(s["w_hot"], 1)

                def update(done):
                    dve.wait_ge(s["w_upd"], done * 2)
                    dve.wait_ge(s["w_mm"], done + 1)
                    v.scalar_tensor_tensor(out=Wt, in0=pw[:, :, 0:P], scalar=0.0, in1=Wt, op0=ALU.is_equal,
                                           op1=ALU.mult).then_inc(s["w_upd"], 1)
                    dve.wait_ge(s["w_upd"], done * 2 + 1)
                    v.tensor_tensor(Wt, Wt, pw[:, :, P:2 * P], ALU.add).then_inc(s["w_upd"], 1)

                if t > 0:
                    dve.wait_ge(s["key_row_ready"], sb_t + lo_t + t)
                mask_keys(lo_t)
                same_keys(lo_t, sb_t + lo_t)
                dst_hots(lo_t, sb_t + lo_t)
                with dve.Fori(lo_t + 1, end_t) as g:
                    w = sb_t + g
                    same_keys(g, w)
                    update(w)
                    dst_hots(g, w)
                update(sb_t + end_t)
                dve.wait_ge(s["w_upd"], (sb_t + end_t) * 2 + 2)
                dve.sem_inc(s["passed"], 1)
            dve.sem_inc(s["w_ready"], 1)

            def root(e, pre, between=None):
                newton = s[pre + "newton"]
                v.tensor_scalar(veps[:], mv[:, 1:2], EPS, None, ALU.add).then_inc(newton, 1)
                dve.wait_ge(newton, e * 12 + 1)
                v.tensor_scalar(half_bits[:], veps[:].bitcast(I32), 1, None, ALU.logical_shift_right).then_inc(newton, 1)
                dve.wait_ge(newton, e * 12 + 2)
                v.tensor_scalar(rs[0][:].bitcast(I32), half_bits[:], -1.0, float(0x5F3759DF), ALU.mult, ALU.add).then_inc(newton, 1)
                for k in range(3):
                    dve.wait_ge(newton, e * 12 + (3 + 3 * k))
                    v.scalar_tensor_tensor(out=rsv[k][:], in0=rs[k][:], scalar=rs[k][:], in1=veps[:], op0=ALU.mult, op1=ALU.mult).then_inc(newton, 1)
                    v.tensor_scalar(rsh[k][:], rs[k][:], -0.5, None, ALU.mult).then_inc(newton, 1)
                    if k == 0 and between is not None:
                        between()
                    dve.wait_ge(newton, e * 12 + (5 + 3 * k))
                    v.tensor_scalar(rs[k + 1][:], rsv[k][:], 3.0, rsh[k][:], ALU.subtract, ALU.mult).then_inc(newton, 1)
                dve.wait_ge(newton, e * 12 + 12)

            def statistics(e, pre, y_in):
                v.bn_stats(st6[:], y_in).then_inc(s[pre + "stats"], 1)
                dve.wait_ge(s[pre + "stats"], e + 1)
                dve.sem_inc(s["passed"], 1)
                v.bn_aggr(mv[:], st6[:]).then_inc(s[pre + "mv"], 1)
                dve.wait_ge(s[pre + "mv"], e + 1)

            def normalise(e, pre, y_in, out_ap):
                statistics(e, pre, y_in)
                root(e, pre)
                return v.tensor_scalar(out_ap, y_in, mv[:, 0:1], rs[3][:], ALU.subtract, ALU.mult)

            def first_norm(t, first=False):
                if not first:
                    dve.wait_ge(s["xn_ready"], t)
                dve.wait_ge(s["x_mm"], t + 1)
                dve.sem_inc(s["passed"], 1)
                v.tensor_tensor(y[:], acc[:, 0:D], X[:, bass.ds(t, 1), :].rearrange("p a d -> p (a d)"), ALU.add).then_inc(s["y_ready"], 1)
                dve.wait_ge(s["y_ready"], t + 1)
                if not first:
                    dve.wait_ge(s["xn_tr"], t)
                    dve.wait_ge(s["xn_stored"], t)
                normalise(t, "n_", y[:], xn[:]).then_inc(s["xn_ready"], 1)
            first_norm(0, first=True)
            with dve.Fori(1, NT) as t:
                first_norm(t)

            def hot(out_ap, g, c, n):
                return v.tensor_tensor(out_ap, iota[:, 0:n].unsqueeze(1).to_broadcast([P, J, n]),
                                       place[:, bass.ds(g, 1), c, :].rearrange("p a j -> p (a j)").unsqueeze(2).to_broadcast([P, J, n]),
                                       ALU.is_equal)

            with dve.Fori(0, NG // 2) as two:
                for half in range(2):
                    g = two * 2 + half
                    dve.wait_ge(s["cnt_mm"], g + 1)
                    dve.sem_inc(s["passed"], 1)
                    hot(hot_s[:, half, :, :], g, 0, NH)
                    hot(hot_n[:, half, :, :], g, 1, P).then_inc(s["hot_ready"], 1)
            dve.wait_ge(s["cnt_mm"], NG + 2)
            v.tensor_scalar(cntm[:], cnt_ps, 1.0, None, ALU.max).then_inc(s["cnt_max"], 1)
            dve.wait_ge(s["cnt_max"], 1)
            v.reciprocal(invd[:], cntm[:]).then_inc(s["inv_ready"], 1)

            def span_hot(g, half):
                dve.wait_ge(s["hot_tr"], g + 1)
                dve.sem_inc(s["passed"], 1)
                hot(hot_s[:, half, :, :], g, 0, NH).then_inc(s["hot_ready"], 1)

            def find(g, half):
                dve.wait_ge(s["inv_found"], g + 2)
                dve.wait_ge(s["inv_mm"], g + 3)
                dve.sem_inc(s["passed"], 1)
                for j in range(J):
                    m = v.scalar_tensor_tensor(out=looked[:, j, :], in0=iota[:, 0:P],
                                               scalar=place[:, bass.ds(g, 1), 1, j:j + 1].rearrange("p a j -> p (a j)"),
                                               in1=hp[half][:, j * P:(j + 1) * P], op0=ALU.is_equal, op1=ALU.mult,
                                               accum_out=ecol[:, bass.ds(g, 1), 1, j:j + 1].rearrange("p a j -> p (a j)"))
                m.then_inc(s["inv_found"], 1)

            span_hot(0, 0)
            span_hot(1, 1)
            with dve.Fori(0, NG // 2 - 1) as two:
                for half in range(2):
                    g = two * 2 + half
                    span_hot(g + 2, half)
                    find(g, half)
            find(NG - 2, 0)
            find(NG - 1, 1)
            dve.wait_ge(s["inv_found"], NG + 2)
            v.tensor_scalar(ecol[:, :, 2, :], ecol[:, :, 1, :], -1.0, None, ALU.mult).then_inc(s["inv_all"], 1)

            dve.wait_ge(s["ld_par"], 48)

            def layer_norm_elu(l, t, steps, out_ap, out_sem):
                def of(a):
                    return a[:, bass.ds(l, 1), :].rearrange("p a d -> p (a d)")
                e, el = l * NT + (t + NT), l * NT + t
                xt = X[:, bass.ds(t, 1), :].rearrange("p a d -> p (a d)")
                bt = base[:, bass.ds(t, 1), :].rearrange("p a d -> p (a d)")
                v.tensor_tensor(ybase[:], bt, of(bias_b), ALU.add).then_inc(s["y_based"], 1)
                dve.wait_ge(s["y_based"], el + 1)
                dve.wait_ge(s["agg_mm"], steps * J + BIAS)
                v.tensor_tensor(y[:], acc[:, 0:D], ybase[:], ALU.add).then_inc(s["y_ready"], 1)
                dve.wait_ge(s["y_ready"], e + 1)
                statistics(e, "n_", y[:])
                root(e, "n_", lambda: v.scalar_tensor_tensor(out=z2[:], in0=y[:], scalar=mv[:, 0:1], in1=of(gamma_b),
                                                             op0=ALU.subtract, op1=ALU.mult).then_inc(s["n_gamma"], 1))
                dve.wait_ge(s["n_gamma"], el + 1)
                v.scalar_tensor_tensor(out=z3[:], in0=z2[:], scalar=rs[3][:], in1=of(beta_b), op0=ALU.mult,
                                       op1=ALU.add).then_inc(s["n_beta"], 1)
                dve.wait_ge(s["n_beta"], el + 1)
                v.tensor_scalar(zm[:], z3[:], 0.0, None, ALU.min).then_inc(s["n_min"], 1)
                v.scalar_tensor_tensor(out=z[:], in0=z3[:], scalar=0.0, in1=xt, op0=ALU.max, op1=ALU.add).then_inc(s["n_elu"], 1)
                dve.wait_ge(s["n_elu"], el + 1)
                if out_sem is not None:
                    dve.wait_ge(s["xn_tr"], e)
                    dve.wait_ge(s["xn_stored"], e)
                dve.wait_ge(s["n_exp"], el + 1)
                m = v.scalar_tensor_tensor(out=out_ap, in0=ze[:], scalar=-1.0, in1=z[:], op0=ALU.add, op1=ALU.add)
                return m.then_inc(s["xn_ready"], 1)

            def store_xn(e, t):
                dve.wait_ge(s["xn_ready"], e + 1)
                dve.sem_inc(s["passed"], 1)
                v.tensor_scalar(X[:, bass.ds(t, 1), :].rearrange("p a d -> p (a d)"), xn[:], 0.0, None, ALU.add).then_inc(s["xn_stored"], 1)

            def products_out(e, t):
                dve.wait_ge(s["h_stored"], e * 16)
                dve.wait_ge(s["h_mm"], e * 3 + 1)
                v.tensor_scalar(hst[:, 0:512], hp[0][:], 0.0, None, ALU.add).then_inc(s["h_out"], 1)
                dve.wait_ge(s["h_mm"], e * 3 + 2)
                v.tensor_scalar(hst[:, 512:1024], hp[1][:], 0.0, None, ALU.add).then_inc(s["h_out"], 1)
                dve.wait_ge(s["h_mm"], e * 3 + 3)
                v.tensor_scalar(base[:, bass.ds(t, 1), :].rearrange("p a d -> p (a d)"), hp[2][:, 0:D],
                                0.0, None, ALU.add).then_inc(s["h_out"], 1)

            def transposed(e):
                dve.wait_ge(s["xn_tr"], e + 1)
                dve.wait_ge(s["h_mm"], e * 3)
                v.tensor_scalar(xnT[:].rearrange("p k n -> p (k n)"), tr[:, 0:D], 0.0, None, ALU.add).then_inc(s["xnT_ready"], 1)

            with dve.Fori(0, L - 1) as l:
                lm = entry(dve, l + T_LM, 0, MAXS)
                dve.wait_ge(s["h_out"], (l + 1) * (3 * NT))
                dve.sem_inc(s["passed"], 1)
                layer_norm_elu(l, 0, lm + entry(dve, T_W + 1, 0, MAXS), xn[:], "xn_ready")
                store_xn(l * NT + NT, 0)
                transposed(l * NT + NT)
                with dve.Fori(1, NT - 1) as t:
                    layer_norm_elu(l, t, lm + entry(dve, t + (T_W + 1), 0, MAXS), xn[:], "xn_ready")
                    store_xn(l * NT + (t + NT), t)
                    products_out(l * NT + (t + NT - 1), t - 1)
                    transposed(l * NT + (t + NT))
                layer_norm_elu(l, NT - 1, lm + entry(dve, T_LM + 1, 0, MAXS), xn[:], "xn_ready")
                store_xn(l * NT + (2 * NT - 1), NT - 1)
                products_out(l * NT + (2 * NT - 2), NT - 2)
                transposed(l * NT + (2 * NT - 1))
                products_out(l * NT + (2 * NT - 1), NT - 1)
            lm = entry(dve, T_LM + L - 1, 0, MAXS)
            dve.wait_ge(s["h_out"], L * 3 * NT)
            dve.wait_ge(s["x1_back"], 16)
            dve.sem_inc(s["passed"], 1)

            def last(t, steps, first=False):
                layer_norm_elu(L - 1, t, steps, xo[:], None)
                dve.wait_ge(s["xn_ready"], t + (L * NT + 1))
                v.tensor_tensor(y[:], xo[:], x1[:, bass.ds(t, 1), :].rearrange("p a d -> p (a d)"), ALU.add).then_inc(s["f_sum"], 1)
                dve.wait_ge(s["f_sum"], t + 1)
                if not first:
                    dve.wait_ge(s["out_stored"], t * 16)
                normalise(t, "f_", y[:], yo[:]).then_inc(s["f_norm"], 1)
            last(0, lm + entry(dve, T_W + 1, 0, MAXS), first=True)
            with dve.Fori(1, NT - 1) as t:
                last(t, lm + entry(dve, t + (T_W + 1), 0, MAXS))
            last(NT - 1, lm + entry(dve, T_LM + 1, 0, MAXS))


def kernel(x, src, dst, edge_type_4, edge_weight, L1_gnn_weights, L1_gnn_roots, L1_gnn_biases, L1_gnn_ln_gamma, L1_gnn_ln_beta):
    import numpy as np
    import concourse.bacc as bacc
    from concourse.bass_utils import run_bass_kernel_spmd

    nc = bacc.Bacc("TRN2", target_bir_lowering=False, num_devices=1)
    inputs = {"x": x, "src": src, "dst": dst, "etype": edge_type_4, "eweight": edge_weight, "weights": L1_gnn_weights,
              "roots": L1_gnn_roots, "biases": L1_gnn_biases, "gammas": L1_gnn_ln_gamma, "betas": L1_gnn_ln_beta}
    arrays, aps = {}, []
    for name, a in inputs.items():
        arrays[name] = np.ascontiguousarray(a)
        aps.append(nc.dram_tensor(name, arrays[name].shape, mybir.dt.from_np(arrays[name].dtype), kind="ExternalInput").ap())
    out = nc.dram_tensor("out", (N, D), F32, kind="ExternalOutput").ap()
    program(nc, *aps, out)
    r = run_bass_kernel_spmd(nc, [arrays], core_ids=[0])
    return r.results[0]["out"]
```
